# Optimizing a Trainium2 kernel written in Bass

```python
import numpy as np
import jax
import jax.numpy as jnp

def _softmax(x, axis=-1):
    return jax.nn.softmax(x, axis=axis)

def _gelu(x):
    return jax.nn.gelu(x, approximate=True)

def _silu(x):
    return jax.nn.silu(x)

def _sigmoid(x):
    return jax.nn.sigmoid(x)

def _layernorm(x, axis=-1, eps=1e-05):
    m = jnp.mean(x, axis=axis, keepdims=True)
    v = jnp.var(x, axis=axis, keepdims=True)
    return (x - m) / jnp.sqrt(v + eps)

def _scatter_add(tgt, idx, src, axis=0):
    return tgt.at[idx].add(src)

def _segment_sum(src, seg, n):
    return jax.ops.segment_sum(src, seg, n)
kernel_name = 'mk_flamingo_gated_d1_seqx_r8_606bfb'

def setup_inputs(seed: int=0):
    np.random.seed(seed)
    _w = jnp.asarray

    def _rec_inputs():
        import jax
        import jax.numpy as jnp
        _rk = jax.random.key(seed)
        x = -0.000125 + 0.9999 * jax.random.normal(jax.random.fold_in(_rk, 1), (4, 256, 256), jnp.float32)
        _lenS = 256 - jax.random.randint(jax.random.fold_in(_rk, 7), (4,), 0, max(1, 256 // 4) + 1, jnp.int32)
        _lenS2 = 256 - jax.random.randint(jax.random.fold_in(_rk, 8), (4,), 0, max(1, 256 // 4) + 1, jnp.int32)
        fside_BxS2xS2_0 = -3.05549e-07 + 0.0199987 * jax.random.normal(jax.random.fold_in(_rk, 11), (4, 256, 256), jnp.float32)
        _ctx_1024P = jax.random.normal(jax.random.fold_in(_rk, 12), (4, 16, 128), jnp.float32)
        _ctx_1024c = jax.random.dirichlet(jax.random.fold_in(_rk, 512), 0.3 * jnp.ones((16,), jnp.float32), (4, 256))
        _ctx_1024t = jnp.einsum('bsk,bkd->bsd', _ctx_1024c, _ctx_1024P)
        _ctx_1024t = _ctx_1024t * jax.lax.rsqrt(jnp.mean(jnp.square(_ctx_1024t)) + 1e-12) * 0.953939
        ctx_1024 = 6.82029e-06 + 0.0200006 * (_ctx_1024t + 0.3 * jax.random.normal(jax.random.fold_in(_rk, 612), (4, 256, 128), jnp.float32))
        _g = jax.random.normal(jax.random.fold_in(_rk, 9001), (2, 1), jnp.float32)
        _g = jnp.sign(_g) * jnp.maximum(jnp.abs(_g), 1.0) + (_g == 0) * 1.0
        g_xattn = _g[0]
        g_ffn = _g[1]
        return (x, fside_BxS2xS2_0, ctx_1024, g_xattn, g_ffn)
    x, fside_BxS2xS2_0, ctx_1024, g_xattn, g_ffn = _rec_inputs()

    def _L0_xattn_setup():
        import jax, jax.numpy as jnp
        import numpy as np
        EPS = 1e-06
        QMAX = 127.0

        def _smooth_quant_linear(x, w):
            amax_x = jnp.max(jnp.abs(x), axis=0)
            amax_w = jnp.max(jnp.abs(w), axis=0)
            s = jnp.sqrt(jnp.maximum(amax_x, EPS) / jnp.maximum(amax_w, EPS))
            s = jnp.maximum(s, EPS)
            xs = x / s
            ws = w * s
            x_scale = jnp.maximum(jnp.max(jnp.abs(xs), axis=-1, keepdims=True), EPS) / QMAX
            w_scale = jnp.maximum(jnp.max(jnp.abs(ws), axis=-1, keepdims=True), EPS) / QMAX
            x_q = jnp.clip(jnp.round(xs / x_scale), -QMAX, QMAX)
            w_q = jnp.clip(jnp.round(ws / w_scale), -QMAX, QMAX)
            return x_q @ w_q.T * x_scale * w_scale.T

        def _expert_forward(xe, guw, dw):
            h = _smooth_quant_linear(xe, guw)
            gate, up = jnp.split(h, 2, axis=-1)
            a = jax.nn.silu(gate) * up
            return _smooth_quant_linear(a, dw)
        key = jax.random.key(seed)
        k1, k2, k3 = jax.random.split(key, 3)
        E, T, D, I = (8, 256, 256, 128)
        x = jax.random.normal(k1, (E, T, D), dtype=jnp.float32)
        gate_up_weight = jax.random.normal(k2, (E, 2 * I, D), dtype=jnp.float32) * 0.02
        down_weight = jax.random.normal(k3, (E, D, I), dtype=jnp.float32) * 0.02
        return {'x': x, 'gate_up_weight': gate_up_weight, 'down_weight': down_weight}
    _L0_xattn_all = _L0_xattn_setup()
    _L0_xattn_in = {k: v for k, v in _L0_xattn_all.items() if k in ()}
    del _L0_xattn_all

    def _L0_ffn_setup():
        import jax, jax.numpy as jnp
        import numpy as np
        CAPACITY_FACTOR = 1.0

        def _top1_gate(x, w_gate):
            S, E = (x.shape[0], w_gate.shape[1])
            capacity = int(CAPACITY_FACTOR * S / E)
            logits = x @ w_gate
            gates = jax.nn.softmax(logits, axis=-1)
            idx1 = jnp.argmax(gates, axis=-1)
            mask1 = jax.nn.one_hot(idx1, E, dtype=gates.dtype)
            locations1 = jnp.cumsum(mask1, axis=0) - mask1
            mask1 = mask1 * (locations1 < capacity)
            locations1_s = jnp.sum(locations1 * mask1, axis=1).astype(jnp.int32)
            gates_masked = gates * mask1
            loc_oh = jax.nn.one_hot(locations1_s, capacity, dtype=gates.dtype) * jnp.sum(mask1, axis=1, keepdims=True)
            combine_weights = jnp.einsum('se,sc->sec', gates_masked, loc_oh)
            dispatch_mask = (combine_weights > 0).astype(gates.dtype)
            return (combine_weights, dispatch_mask)
        key = jax.random.key(seed)
        k1, k2, k3, k4 = jax.random.split(key, 4)
        B, T, D, E, F = (4, 256, 256, 8, 1024)
        hidden_states = jax.random.normal(k1, (B, T, D), dtype=jnp.float32)
        w_gate = jax.random.normal(k2, (D, E), dtype=jnp.float32) * 0.02
        w1 = jax.random.normal(k3, (E, D, F), dtype=jnp.float32) * 0.02
        w2 = jax.random.normal(k4, (E, F, D), dtype=jnp.float32) * 0.02
        return {'hidden_states': hidden_states, 'w_gate': w_gate, 'w1': w1, 'w2': w2}
    _L0_ffn_all = _L0_ffn_setup()
    _L0_ffn_in = {k: v for k, v in _L0_ffn_all.items() if k in ('w_gate', 'w1', 'w2')}
    del _L0_ffn_all
    return {'x': x, 'fside_BxS2xS2_0': fside_BxS2xS2_0, 'ctx_1024': ctx_1024, 'g_xattn': g_xattn, 'g_ffn': g_ffn, 'L0_ffn_w_gate': _L0_ffn_in['w_gate'], 'L0_ffn_w1': _L0_ffn_in['w1'], 'L0_ffn_w2': _L0_ffn_in['w2']}

def reference(x, fside_BxS2xS2_0, ctx_1024, g_xattn, g_ffn, L0_ffn_w_gate, L0_ffn_w1, L0_ffn_w2):
    import jax
    import jax.numpy as jnp

    def _L0_xattn_ref(x, gate_up_weight, down_weight):
        import jax, jax.numpy as jnp
        import numpy as np
        EPS = 1e-06
        QMAX = 127.0

        def _smooth_quant_linear(x, w):
            amax_x = jnp.max(jnp.abs(x), axis=0)
            amax_w = jnp.max(jnp.abs(w), axis=0)
            s = jnp.sqrt(jnp.maximum(amax_x, EPS) / jnp.maximum(amax_w, EPS))
            s = jnp.maximum(s, EPS)
            xs = x / s
            ws = w * s
            x_scale = jnp.maximum(jnp.max(jnp.abs(xs), axis=-1, keepdims=True), EPS) / QMAX
            w_scale = jnp.maximum(jnp.max(jnp.abs(ws), axis=-1, keepdims=True), EPS) / QMAX
            x_q = jnp.clip(jnp.round(xs / x_scale), -QMAX, QMAX)
            w_q = jnp.clip(jnp.round(ws / w_scale), -QMAX, QMAX)
            return x_q @ w_q.T * x_scale * w_scale.T

        def _expert_forward(xe, guw, dw):
            h = _smooth_quant_linear(xe, guw)
            gate, up = jnp.split(h, 2, axis=-1)
            a = jax.nn.silu(gate) * up
            return _smooth_quant_linear(a, dw)
        return jax.vmap(_expert_forward)(x, gate_up_weight, down_weight)

    def _L0_ffn_ref(hidden_states, w_gate, w1, w2):
        import jax, jax.numpy as jnp
        import numpy as np
        CAPACITY_FACTOR = 1.0

        def _top1_gate(x, w_gate):
            S, E = (x.shape[0], w_gate.shape[1])
            capacity = int(CAPACITY_FACTOR * S / E)
            logits = x @ w_gate
            gates = jax.nn.softmax(logits, axis=-1)
            idx1 = jnp.argmax(gates, axis=-1)
            mask1 = jax.nn.one_hot(idx1, E, dtype=gates.dtype)
            locations1 = jnp.cumsum(mask1, axis=0) - mask1
            mask1 = mask1 * (locations1 < capacity)
            locations1_s = jnp.sum(locations1 * mask1, axis=1).astype(jnp.int32)
            gates_masked = gates * mask1
            loc_oh = jax.nn.one_hot(locations1_s, capacity, dtype=gates.dtype) * jnp.sum(mask1, axis=1, keepdims=True)
            combine_weights = jnp.einsum('se,sc->sec', gates_masked, loc_oh)
            dispatch_mask = (combine_weights > 0).astype(gates.dtype)
            return (combine_weights, dispatch_mask)
        B, T, D = hidden_states.shape
        x = hidden_states.reshape(-1, D)
        combine_weights, dispatch_mask = _top1_gate(x, w_gate)
        dispatched = jnp.einsum('sec,sm->ecm', dispatch_mask, x)
        h = jax.nn.gelu(jnp.einsum('ecd,edf->ecf', dispatched, w1))
        expert_out = jnp.einsum('ecf,efd->ecd', h, w2)
        combined = jnp.einsum('sec,ecm->sm', combine_weights, expert_out)
        return combined.reshape(B, T, D)
    x = x + jnp.tanh(g_xattn[0]) * _L0_xattn_ref(_layernorm(x, axis=-1), fside_BxS2xS2_0, ctx_1024)
    x = x + jnp.tanh(g_ffn[0]) * _L0_ffn_ref(_layernorm(x, axis=-1), L0_ffn_w_gate, L0_ffn_w1, L0_ffn_w2)
    return x

_drawn_inputs = setup_inputs


def setup_inputs(seed=0):
    import zlib

    import numpy as np

    out = dict(_drawn_inputs(seed))
    spreads = {}
    factors = {'fside_BxS2xS2_0': 6.183,
     'ctx_1024': 6.156,
     'L0_ffn_w_gate': 3.058,
     'L0_ffn_w1': 2.917,
     'L0_ffn_w2': 2.85}
    for name, (base, spread) in spreads.items():
        noise = np.random.default_rng([zlib.crc32(name.encode()), seed]).standard_normal(out[name].shape)
        drawn = base * np.exp(spread * noise) if base else spread * noise
        out[name] = jnp.asarray(drawn.astype(out[name].dtype))
    for name, factor in factors.items():
        out[name] = (out[name] * factor).astype(out[name].dtype)
    return out
```

```python
import concourse.bass as bass
from concourse import mybir
from contextlib import ExitStack


def gated_smoothquant_moe_kernel(nc, x_in, ctx_in, down_in, g_xattn, g_ffn, w_gate, w1, w2, scratch, out):
    F32 = mybir.dt.float32
    BF16 = mybir.dt.bfloat16
    I32 = mybir.dt.int32
    ALU = mybir.AluOpType
    ACT = mybir.ActivationFunctionType
    AX = mybir.AxisListType.X

    P = 128
    B, T, D = x_in.shape
    I = down_in.shape[2]
    E, _, F = w1.shape
    J = T // P
    K = D // P
    C = B * T // E
    NF = F // P
    assert (T, D, I, C) == (256, 256, P, P) and ctx_in.shape[1] == 2 * I
    EPS, LN_EPS, QMAX = 1e-6, 1e-5, 127.0
    ROUND = 12582912.0
    DROPPED = 4096.0
    MEAN, RSTD, TOKEN, LOGIT = D, D + 1, D + 2, D + 3
    ROW = LOGIT + E
    NW = 6

    ctx = ExitStack()
    with ctx:
        def sb(name, shape, dt=F32):
            return ctx.enter_context(nc.sbuf_tensor(name, shape, dt))

        def ps(name, shape, dt=F32):
            return ctx.enter_context(nc.psum_tensor(name, shape, dt))

        def sem(name):
            return ctx.enter_context(nc.semaphore(name))

        x = sb("x", [P, B, J, D])
        cw = sb("cw", [P, B, J, D])
        dw = sb("dw", [P, B, K, I])
        wg = sb("wg", [P, K, E])
        ident = sb("ident", [P, P])
        identb = sb("identb", [P, P], BF16)
        upper = sb("upper", [P, P], BF16)
        upper_eq = sb("upper_eq", [P, P], BF16)
        ones = sb("ones", [P, P], BF16)
        rank = sb("rank", [P, J, E])
        half = sb("half", [P, K])
        mhalf = sb("mhalf", [P, J])
        rbias = sb("rbias", [P, 1])
        gates = sb("gates", [P, 2])
        tg = sb("tg", [P, 2])
        empty = sb("empty", [P, E, ROW])
        st1 = sb("st1", [P, J, 6])
        mv1 = sb("mv1", [P, J, 2])
        ve1 = sb("ve1", [P, J])
        rs1 = sb("rs1", [P, J])
        xn = sb("xn", [P, J, D])
        am1 = sb("am1", [P, 2 * K])
        rw1 = sb("rw1", [P, K])
        ra1 = sb("ra1", [P, K])
        root1 = sb("root1", [P, K])
        sc1 = sb("sc1", [P, 2 * K])
        xs1 = sb("xs1", [P, 2 * K, T])
        am2 = sb("am2", [P, 2 * J])
        q1s = sb("q1s", [P, 2, 2 * J])
        q1r = sb("q1r", [P, 2 * J])
        qf1 = sb("qf1", [P, 2 * J, D])
        qb1 = sb("qb1", [P, 2 * J, D], BF16)
        qT1 = sb("qT1", [P, 2 * K, T], BF16)
        xrow = sb("xrow", [P, T])
        g_sb = sb("g_sb", [P, T])
        u_sb = sb("u_sb", [P, T])
        sg = sb("sg", [P, T])
        a_sb = sb("a_sb", [P, T])
        dT = sb("dT", [P, B, D])
        amd = sb("amd", [P, B])
        rwd = sb("rwd", [P, B])
        ama = sb("ama", [P, 1])
        ra2 = sb("ra2", [P, 1])
        root2 = sb("root2", [P, 1])
        sc3 = sb("sc3", [P, 2])
        aw = sb("aw", [P, 2, T])
        am4 = sb("am4", [P, 2 * J])
        q2s = sb("q2s", [P, 2 * J])
        q2r = sb("q2r", [P, 2 * J])
        q2g = sb("q2g", [P, J])
        qf2 = sb("qf2", [P, 2 * J, I])
        qb2 = sb("qb2", [P, 2 * J, I], BF16)
        qT2 = sb("qT2", [P, 2, T], BF16)
        drow = sb("drow", [P, D])
        y1 = sb("y1", [P, J, D])
        row = sb("row", [P, B, J, ROW])
        st2 = sb("st2", [P, J, 6])
        mv2 = sb("mv2", [P, J, 2])
        ve2 = sb("ve2", [P, J])
        xn2 = sb("xn2", [P, J, D])
        xn2T = sb("xn2T", [P, K, T])
        lmax = sb("lmax", [P, J])
        prio = sb("prio", [P, J, E])
        pmax = sb("pmax", [P, J])
        base = sb("base", [P, J])
        onehot = sb("onehot", [P, B, J, E], BF16)
        locm = sb("locm", [P, J, E])
        loc = sb("loc", [P, J])
        over = sb("over", [P, J])
        where_ = sb("where_", [P, J])
        slot = sb("slot", [P, B, J], I32)
        w1_sb = sb("w1_sb", [P, NW, K, F])
        w2_sb = sb("w2_sb", [P, NW, NF, D])
        gr = sb("gr", [P, E, ROW])
        ex = sb("ex", [P, E, E])
        zs = sb("zs", [P, E])
        zr = sb("zr", [P, E])
        gt = sb("gt", [P, E])
        xg = sb("xg", [P, 2, D])
        xgT = sb("xgT", [P, 2, K, C])
        hs = sb("hs", [P, 2, NF, C])
        yo = sb("yo", [P, 2, D])

        bk = [ps(f"bk{i}", [P, 2, 512]) for i in range(4)]
        T1 = bk[0]
        T2 = bk[1]
        T3 = bk[2][:, 0, :]
        R5 = bk[2][:, 1, :]
        R6 = bk[3][:, 0, :]
        R7 = bk[3][:, 1, :]
        HB = [bk[0], bk[1]]
        XT = [bk[2][:, 0, :], bk[2][:, 1, :]]
        YB = [bk[3][:, 0, :], bk[3][:, 1, :]]

        x_here = [sem(f"x_here{b}") for b in range(B)]
        cw_here = [sem(f"cw_here{b}") for b in range(B)]
        small_here = sem("small_here")
        dw_here = sem("dw_here")
        scratch_clear = sem("scratch_clear")
        w_here = [sem(f"w_here{i}") for i in range(NW)]
        plain_out = sem("plain_out")
        rows_scattered = sem("rows_scattered")
        rows_here = sem("rows_here")
        rest_here = sem("rest_here")
        out_scattered = [sem("out_scattered0"), sem("out_scattered1")]
        consts = sem("consts")
        pool_c = sem("pool_c")
        dve_c = sem("dve_c")
        dve_consts = sem("dve_consts")
        tanh_ready = sem("tanh_ready")
        var1_ready, rstd1_ready, xn_ready = sem("var1_ready"), sem("rstd1_ready"), sem("xn_ready")
        t1_ready, ratio1_ready, root1_ready = sem("t1_ready"), sem("ratio1_ready"), sem("root1_ready")
        scale1_ready, scaled1, t2_ready = sem("scale1_ready"), sem("scaled1"), sem("t2_ready")
        recip1_ready, quant1, rounded1 = sem("recip1_ready"), sem("quant1"), sem("rounded1")
        t3_ready, moved1, row1_ready, row1_moved = sem("t3_ready"), sem("moved1"), sem("row1_ready"), sem("row1_moved")
        h_ready, gate_ready, up_ready = sem("h_ready"), sem("gate_ready"), sem("up_ready")
        silu_ready, act_ready = sem("silu_ready"), sem("act_ready")
        dT_ready, dT_moved = sem("dT_ready"), sem("dT_moved")
        ratio2_ready, root2_ready, scale2_ready = sem("ratio2_ready"), sem("root2_ready"), sem("scale2_ready")
        scaled2, t4_ready, recip2_ready = sem("scaled2"), sem("t4_ready"), sem("recip2_ready")
        quant2, rounded2, t5_ready, moved2 = sem("quant2"), sem("rounded2"), sem("t5_ready"), sem("moved2")
        row2_ready, row2_moved, o_ready, y1_ready = sem("row2_ready"), sem("row2_moved"), sem("o_ready"), sem("y1_ready")
        x1_ready, var2_ready, rstd2_ready, xn2_ready = sem("x1_ready"), sem("var2_ready"), sem("rstd2_ready"), sem("xn2_ready")
        t6_ready, moved3, logits_ready = sem("t6_ready"), sem("moved3"), sem("logits_ready")
        onehot_ready, loc_ready, loc_read, slot_ready = sem("onehot_ready"), sem("loc_ready"), sem("loc_read"), sem("slot_ready")
        exp_ready, gt_ready = sem("exp_ready"), sem("gt_ready")
        xg_ready, xT_ready, xgT_ready = sem("xg_ready"), sem("xT_ready"), sem("xgT_ready")
        hid_ready, gelu_ready, y_ready, y_used = sem("hid_ready"), sem("gelu_ready"), sem("y_ready"), sem("y_used")

        block = ctx.enter_context(nc.Block())

        @block.sync
        def _(sp):
            for b in range(B):
                sp.dma_start(x[:, b], x_in[b].rearrange("(p j) d -> p j d", j=J)).then_inc(x_here[b], 16)
                sp.dma_start(cw[:, b], ctx_in[b].rearrange("(j p) d -> p j d", p=P)).then_inc(cw_here[b], 16)
                if b == 0:
                    sp.dma_start(dw[:], down_in.rearrange("b (k p) i -> p b k i", p=P)).then_inc(dw_here, 16)
                    sp.dma_start(gates[:, 0:1], g_xattn.partition_broadcast(P)).then_inc(small_here, 16)
                    sp.dma_start(gates[:, 1:2], g_ffn.partition_broadcast(P)).then_inc(small_here, 16)
                    sp.dma_start(wg[:], w_gate.rearrange("(k p) e -> p k e", p=P)).then_inc(small_here, 16)
            sp.wait_ge(consts, 2)
            sp.dma_start(scratch.rearrange("(e p) r -> p e r", p=P), empty[:]).then_inc(scratch_clear, 16)

            def load(e):
                if e >= 1:
                    sp.wait_ge(w_here[(e - 1) % NW], 32 * ((e - 1) // NW + 1))
                if e >= NW:
                    sp.wait_ge(y_ready, e - NW + 1)
                sp.dma_start(w1_sb[:, e % NW], w1[e].rearrange("(p k) f -> p k f", k=K)).then_inc(w_here[e % NW], 16)
                sp.dma_start(w2_sb[:, e % NW], w2[e].rearrange("(p n) d -> p n d", n=NF)).then_inc(w_here[e % NW], 16)

            for e in range(NW):
                load(e)
            for b in range(B):
                sp.wait_ge(x1_ready, b + 1)
                sp.dma_start(out[b].rearrange("(p j) d -> p j d", j=J), row[:, b, :, 0:D]).then_inc(plain_out, 16)
            for e in range(NW, E):
                load(e)
            for n in range(2):
                sp.wait_ge(out_scattered[n], 16 * (E // 2))

        @block.gpsimd
        def _(pool):
            nc.gpsimd.memset(ident[:], 0.0).then_inc(pool_c, 1)
            nc.gpsimd.memset(upper[:], 1.0).then_inc(pool_c, 1)
            nc.gpsimd.memset(upper_eq[:], 1.0).then_inc(pool_c, 1)
            nc.gpsimd.memset(empty[:], 0.0).then_inc(pool_c, 1)
            nc.gpsimd.memset(identb[:], 0.0).then_inc(pool_c, 1)
            pool.wait_ge(pool_c, 5)
            nc.gpsimd.affine_select(out=ident[:], in_=ident[:], compare_op=ALU.not_equal, fill=1.0, base=0,
                                    pattern=[[-1, P]], channel_multiplier=1).then_inc(consts, 1)
            nc.gpsimd.iota(empty[:, :, TOKEN:TOKEN + 1].bitcast(I32), pattern=[[0, E]], base=1 << 20,
                           channel_multiplier=0).then_inc(consts, 1)
            nc.gpsimd.affine_select(out=identb[:], in_=identb[:], compare_op=ALU.not_equal, fill=1.0, base=0,
                                    pattern=[[-1, P]], channel_multiplier=1).then_inc(consts, 1)
            nc.gpsimd.affine_select(out=upper[:], in_=upper[:], compare_op=ALU.is_gt, fill=0.0, base=0,
                                    pattern=[[1, P]], channel_multiplier=-1).then_inc(consts, 1)
            nc.gpsimd.affine_select(out=upper_eq[:], in_=upper_eq[:], compare_op=ALU.is_ge, fill=0.0, base=0,
                                    pattern=[[1, P]], channel_multiplier=-1).then_inc(consts, 1)
            nc.gpsimd.iota(rank[:], pattern=[[0, J], [-1, E]], base=E, channel_multiplier=0,
                           allow_small_or_imprecise_dtypes=True).then_inc(consts, 1)
            nc.gpsimd.iota(row[:, :, :, TOKEN:TOKEN + 1].bitcast(I32), pattern=[[T, B], [1, J]], base=0,
                           channel_multiplier=J).then_inc(consts, 1)

            def rstd1(b):
                pool.wait_ge(var1_ready, b + 1)
                if b >= 1:
                    pool.wait_ge(xn_ready, b)
                nc.gpsimd.tensor_tensor(rs1[:], ve1[:], mhalf[:], ALU.pow).then_inc(rstd1_ready, 1)

            def smooth1(b):
                pool.wait_ge(ratio1_ready, b + 1)
                nc.gpsimd.tensor_tensor(root1[:], ra1[:], half[:], ALU.pow).then_inc(root1_ready, 1)

            def round1(b):
                pool.wait_ge(quant1, b + 1)
                if b >= 1:
                    pool.wait_ge(t3_ready, b)
                nc.gpsimd.tensor_scalar(qb1[:], qf1[:], -ROUND, 1.0, ALU.add, ALU.mult).then_inc(rounded1, 1)

            def act_product(b):
                pool.wait_ge(silu_ready, b + 1)
                pool.wait_ge(up_ready, b + 1)
                if b >= 1:
                    pool.wait_ge(scaled2, b)
                nc.gpsimd.tensor_tensor(a_sb[:], sg[:], u_sb[:], ALU.mult).then_inc(act_ready, 1)

            def smooth2(b):
                pool.wait_ge(ratio2_ready, b + 1)
                nc.gpsimd.tensor_tensor(root2[:], ra2[:], half[:, 0:1], ALU.pow).then_inc(root2_ready, 1)

            def round2(b):
                pool.wait_ge(quant2, b + 1)
                if b >= 1:
                    pool.wait_ge(t5_ready, b)
                nc.gpsimd.tensor_scalar(qb2[:], qf2[:], -ROUND, 1.0, ALU.add, ALU.mult).then_inc(rounded2, 1)

            def residual(b):
                pool.wait_ge(y1_ready, b + 1)
                nc.gpsimd.tensor_tensor(row[:, b, :, 0:D], x[:, b], y1[:], ALU.add).then_inc(x1_ready, 1)

            def rstd2(b):
                pool.wait_ge(var2_ready, b + 1)
                nc.gpsimd.tensor_tensor(row[:, b, :, RSTD], ve2[:], mhalf[:], ALU.pow).then_inc(rstd2_ready, 1)

            def scatter(b):
                pool.wait_ge(slot_ready, b + 1)
                if b == 0:
                    pool.wait_ge(scratch_clear, 16)
                    pool.wait_ge(consts, 7)
                for j in range(J):
                    nc.gpsimd.indirect_dma_start(
                        scratch, bass.IndirectOffsetOnAxis(ap=slot[:, b, j:j + 1], axis=0), row[:, b, j, :], None,
                        bounds_check=E * C - 1, oob_is_err=False).then_inc(rows_scattered, 16)

            pool.wait_ge(dve_consts, 1)
            for s in range(B + 1):
                if s < B:
                    rstd1(s)
                if s >= 1:
                    act_product(s - 1)
                if s < B:
                    smooth1(s)
                if s >= 1:
                    smooth2(s - 1)
                    round2(s - 1)
                if s < B:
                    round1(s)
                if s >= 1:
                    residual(s - 1)
                    rstd2(s - 1)
                    scatter(s - 1)

            out_rows = out.rearrange("b t d -> (b t) d")
            for e in range(E):
                pool.wait_ge(y_ready, e + 1)
                if e == 0:
                    pool.wait_ge(plain_out, 16 * B)
                nc.gpsimd.indirect_dma_start(
                    out_rows, bass.IndirectOffsetOnAxis(ap=gr[:, e, TOKEN:TOKEN + 1].bitcast(I32), axis=0),
                    yo[:, e % 2, :], None, bounds_check=B * T - 1, oob_is_err=False).then_inc(out_scattered[e % 2], 16)

        @block.scalar
        def _(act):
            act.wait_ge(small_here, 48)
            nc.scalar.activation(tg[:], gates[:], ACT.Tanh).then_inc(tanh_ready, 1)
            act.wait_ge(dve_consts, 1)

            def scale1(b):
                act.wait_ge(scale1_ready, b + 1)
                if b >= 1:
                    act.wait_ge(t2_ready, b)
                for c in range(2 * K):
                    last = nc.scalar.activation(xs1[:, c], T1[:, c // K, (c % K) * T:(c % K + 1) * T], ACT.Identity,
                                                scale=sc1[:, c:c + 1])
                last.then_inc(scaled1, 1)

            def quantise1(b):
                act.wait_ge(recip1_ready, b + 1)
                if b >= 1:
                    act.wait_ge(rounded1, b)
                for c in range(2 * J):
                    last = nc.scalar.activation(qf1[:, c], T2[:, c // J, (c % J) * D:(c % J + 1) * D], ACT.Identity,
                                                scale=q1r[:, c:c + 1], bias=rbias[:, 0:1])
                last.then_inc(quant1, 1)

            def move1(b):
                act.wait_ge(row1_ready, b + 1)
                if b >= 1:
                    act.wait_ge(up_ready, b)
                nc.scalar.activation(xrow[:], R6[:, 0:T], ACT.Copy).then_inc(row1_moved, 1)
                act.wait_ge(t3_ready, b + 1)
                if b >= 1:
                    act.wait_ge(h_ready, b)
                nc.scalar.activation(qT1[:].rearrange("p a t -> p (a t)").bitcast(F32), T3, ACT.Copy).then_inc(moved1, 1)

            def silu(b):
                act.wait_ge(gate_ready, b + 1)
                if b >= 1:
                    act.wait_ge(act_ready, b)
                nc.scalar.activation(sg[:], g_sb[:], ACT.Silu).then_inc(silu_ready, 1)

            def scale2(b):
                act.wait_ge(scale2_ready, b + 1)
                if b >= 1:
                    act.wait_ge(t4_ready, b)
                nc.scalar.activation(aw[:, 0], a_sb[:], ACT.Identity, scale=sc3[:, 0:1])
                nc.scalar.activation(aw[:, 1], dT[:, b], ACT.Identity, scale=sc3[:, 1:2]).then_inc(scaled2, 1)

            def quantise2(b):
                act.wait_ge(recip2_ready, b + 1)
                if b >= 1:
                    act.wait_ge(rounded2, b)
                for c in range(2 * J):
                    last = nc.scalar.activation(qf2[:, c], R7[:, c * I:(c + 1) * I], ACT.Identity,
                                                scale=q2r[:, c:c + 1], bias=rbias[:, 0:1])
                last.then_inc(quant2, 1)

            def move2(b):
                act.wait_ge(row2_ready, b + 1)
                if b >= 1:
                    act.wait_ge(y1_ready, b)
                nc.scalar.activation(drow[:], R6[:, 0:D], ACT.Copy).then_inc(row2_moved, 1)
                act.wait_ge(t5_ready, b + 1)
                if b >= 1:
                    act.wait_ge(o_ready, b)
                nc.scalar.activation(qT2[:].rearrange("p a t -> p (a t)").bitcast(F32), R7[:, 0:T],
                                     ACT.Copy).then_inc(moved2, 1)

            def move3(b):
                act.wait_ge(t6_ready, b + 1)
                if b >= 1:
                    act.wait_ge(logits_ready, b)
                nc.scalar.activation(xn2T[:].rearrange("p k t -> p (k t)"), R5, ACT.Copy).then_inc(moved3, 1)

            for s in range(B + 1):
                if s >= 1:
                    silu(s - 1)
                if s < B:
                    scale1(s)
                if s >= 1:
                    scale2(s - 1)
                    quantise2(s - 1)
                if s < B:
                    quantise1(s)
                if s < B:
                    move1(s)
                if s >= 1:
                    move2(s - 1)
                if s >= 1:
                    move3(s - 1)

            sc_rows = scratch.rearrange("(e p) r -> p e r", p=P)
            act.wait_ge(rows_scattered, 16 * B * J)
            act.dma_start(gr[:, 0:1], sc_rows[:, 0:1]).then_inc(rows_here, 16)
            act.dma_start(gr[:, 1:E], sc_rows[:, 1:E]).then_inc(rest_here, 16)
            act.wait_ge(rows_here, 16)
            act.wait_ge(rest_here, 16)
            nc.scalar.activation(ex[:], gr[:, :, LOGIT:ROW], ACT.Exp).then_inc(exp_ready, 1)
            for e in range(E):
                for m in range(2):
                    act.wait_ge(hid_ready, 2 * e + m + 1)
                    if e >= 2:
                        act.wait_ge(y_used, e - 1)
                    nc.scalar.activation(hs[:, e % 2, 4 * m:4 * m + 4].rearrange("p n c -> p (n c)"),
                                         HB[e % 2][:, m, :], ACT.Gelu_apprx_tanh).then_inc(gelu_ready, 1)

        @block.vector
        def _(dve):
            chain = [0]

            def link(ins):
                chain[0] += 1
                ins.then_inc(dve_c, 1)
                dve.wait_ge(dve_c, chain[0])

            nc.vector.memset(half[:], 0.5)
            nc.vector.memset(mhalf[:], -0.5)
            nc.vector.memset(ones[:], 1.0)
            nc.vector.memset(rbias[:], ROUND).then_inc(dve_consts, 1)

            def stats1(b):
                dve.wait_ge(x_here[b], 16)
                for j in range(J):
                    ins = nc.vector.bn_stats(st1[:, j], x[:, b, j])
                link(ins)
                for j in range(J):
                    ins = nc.vector.bn_aggr(mv1[:, j], st1[:, j])
                link(ins)
                nc.vector.tensor_scalar(ve1[:], mv1[:, :, 1], LN_EPS, None, ALU.add).then_inc(var1_ready, 1)

            def norm1(b):
                dve.wait_ge(rstd1_ready, b + 1)
                if b >= 1:
                    dve.wait_ge(t1_ready, b)
                for j in range(J):
                    ins = nc.vector.tensor_scalar(xn[:, j], x[:, b, j], mv1[:, j, 0:1], rs1[:, j:j + 1],
                                                  ALU.subtract, ALU.mult)
                ins.then_inc(xn_ready, 1)

            def amax1(b):
                dve.wait_ge(t1_ready, b + 1)
                link(nc.vector.tensor_reduce(am1[:], T1[:].rearrange("p a (k t) -> p (a k) t", k=K), AX, ALU.max,
                                             apply_absolute_value=True))
                link(nc.vector.tensor_scalar(am1[:], am1[:], EPS, None, ALU.max))
                link(nc.vector.reciprocal(rw1[:], am1[:, K:2 * K]))
                nc.vector.tensor_tensor(ra1[:], am1[:, 0:K], rw1[:], ALU.mult).then_inc(ratio1_ready, 1)

            def smooth1(b):
                dve.wait_ge(root1_ready, b + 1)
                link(nc.vector.tensor_scalar(sc1[:, K:2 * K], root1[:], EPS, None, ALU.max))
                nc.vector.reciprocal(sc1[:, 0:K], sc1[:, K:2 * K]).then_inc(scale1_ready, 1)

            def scales1(b):
                dve.wait_ge(t2_ready, b + 1)
                link(nc.vector.tensor_reduce(am2[:], T2[:].rearrange("p a (j d) -> p (a j) d", j=J), AX, ALU.max,
                                             apply_absolute_value=True))
                link(nc.vector.tensor_scalar(q1s[:, b % 2], am2[:], EPS, 1.0 / QMAX, ALU.max, ALU.mult))
                nc.vector.reciprocal(q1r[:], q1s[:, b % 2]).then_inc(recip1_ready, 1)

            def down_amax():
                for b in range(B):
                    dve.wait_ge(dT_ready, b + 1)
                    nc.vector.tensor_reduce(amd[:, b:b + 1], R7[:, 0:D], AX, ALU.max, apply_absolute_value=True)
                    ins = nc.vector.tensor_copy(dT[:, b], R7[:, 0:D])
                    ins.then_inc(dT_moved, 1)
                dve.wait_ge(dT_moved, B)
                link(nc.vector.tensor_scalar(amd[:], amd[:], EPS, None, ALU.max))
                link(nc.vector.reciprocal(rwd[:], amd[:]))

            def gate_up(b):
                dve.wait_ge(h_ready, b + 1)
                dve.wait_ge(row1_moved, b + 1)
                if b >= 1:
                    dve.wait_ge(silu_ready, b)
                    dve.wait_ge(act_ready, b)
                for h, (dst, done) in enumerate(((g_sb, gate_ready), (u_sb, up_ready))):
                    nc.vector.scalar_tensor_tensor(out=dst[:], in0=T3[:, h * T:(h + 1) * T],
                                                   scalar=q1s[:, b % 2, J + h:J + h + 1], in1=xrow[:],
                                                   op0=ALU.mult, op1=ALU.mult).then_inc(done, 1)

            def amax2(b):
                dve.wait_ge(act_ready, b + 1)
                link(nc.vector.tensor_reduce(ama[:], a_sb[:], AX, ALU.max, apply_absolute_value=True))
                nc.vector.tensor_scalar(ra2[:], ama[:], EPS, rwd[:, b:b + 1], ALU.max, ALU.mult).then_inc(ratio2_ready, 1)

            def smooth2(b):
                dve.wait_ge(root2_ready, b + 1)
                link(nc.vector.tensor_scalar(sc3[:, 1:2], root2[:], EPS, None, ALU.max))
                nc.vector.reciprocal(sc3[:, 0:1], sc3[:, 1:2]).then_inc(scale2_ready, 1)

            def scales2(b):
                dve.wait_ge(t4_ready, b + 1)
                link(nc.vector.tensor_reduce(am4[:], R7.rearrange("p (c i) -> p c i", i=I), AX, ALU.max,
                                             apply_absolute_value=True))
                link(nc.vector.tensor_scalar(q2s[:], am4[:], EPS, 1.0 / QMAX, ALU.max, ALU.mult))
                nc.vector.reciprocal(q2r[:], q2s[:]).then_inc(recip2_ready, 1)
                if b == 0:
                    dve.wait_ge(tanh_ready, 1)
                link(nc.vector.tensor_scalar(q2g[:], q2s[:, 0:J], tg[:, 0:1], None, ALU.mult))

            def expert_out(b):
                dve.wait_ge(o_ready, b + 1)
                dve.wait_ge(row2_moved, b + 1)
                if b >= 1:
                    dve.wait_ge(x1_ready, b)
                for j in range(J):
                    ins = nc.vector.scalar_tensor_tensor(out=y1[:, j], in0=R7[:, j * D:(j + 1) * D],
                                                         scalar=q2g[:, j:j + 1], in1=drow[:], op0=ALU.mult, op1=ALU.mult)
                ins.then_inc(y1_ready, 1)

            def stats2(b):
                dve.wait_ge(x1_ready, b + 1)
                for j in range(J):
                    ins = nc.vector.bn_stats(st2[:, j], row[:, b, j, 0:D])
                link(ins)
                for j in range(J):
                    ins = nc.vector.bn_aggr(mv2[:, j], st2[:, j])
                link(ins)
                nc.vector.tensor_scalar(ve2[:], mv2[:, :, 1], LN_EPS, None, ALU.add).then_inc(var2_ready, 1)
                link(nc.vector.tensor_copy(row[:, b, :, MEAN], mv2[:, :, 0]))

            def norm2(b):
                dve.wait_ge(rstd2_ready, b + 1)
                if b >= 1:
                    dve.wait_ge(t6_ready, b)
                for j in range(J):
                    ins = nc.vector.tensor_scalar(xn2[:, j], row[:, b, j, 0:D], row[:, b, j, MEAN:MEAN + 1],
                                                  row[:, b, j, RSTD:RSTD + 1], ALU.subtract, ALU.mult)
                ins.then_inc(xn2_ready, 1)

            def choose(b):
                dve.wait_ge(logits_ready, b + 1)
                if b == 0:
                    dve.wait_ge(consts, 7)
                lg = R5[:, 0:J * E].rearrange("p (j e) -> p j e", e=E)
                link(nc.vector.tensor_reduce(lmax[:], lg, AX, ALU.max))
                lrel = row[:, b, :, LOGIT:ROW]
                link(nc.vector.tensor_tensor(lrel, lg, lmax[:].unsqueeze(2).to_broadcast([P, J, E]), ALU.subtract))
                link(nc.vector.scalar_tensor_tensor(out=prio[:], in0=lrel, scalar=0.0, in1=rank[:],
                                                    op0=ALU.is_ge, op1=ALU.mult))
                link(nc.vector.tensor_reduce(pmax[:], prio[:], AX, ALU.max))
                nc.vector.tensor_tensor(onehot[:, b], prio[:], pmax[:].unsqueeze(2).to_broadcast([P, J, E]),
                                        ALU.is_equal).then_inc(onehot_ready, 1)
                nc.vector.tensor_scalar(base[:], pmax[:], -float(C), float(C * E), ALU.mult, ALU.add)

            def place(b):
                dve.wait_ge(loc_ready, b + 1)
                dve.wait_ge(onehot_ready, b + 1)
                ins = nc.vector.tensor_tensor(locm[:], R5[:, 32:32 + J * E].rearrange("p (j e) -> p j e", e=E),
                                              onehot[:, b], ALU.mult)
                ins.then_inc(loc_read, 1)
                dve.wait_ge(loc_read, b + 1)
                link(nc.vector.tensor_reduce(loc[:], locm[:], AX, ALU.add))
                nc.vector.tensor_scalar(over[:], loc[:], float(C), DROPPED, ALU.is_ge, ALU.mult)
                link(nc.vector.tensor_tensor(where_[:], loc[:], base[:], ALU.add))
                nc.vector.tensor_tensor(slot[:, b], where_[:], over[:], ALU.add).then_inc(slot_ready, 1)

            for s in range(B + 1):
                if s < B:
                    stats1(s)
                if s >= 1:
                    gate_up(s - 1)
                if s < B:
                    norm1(s)
                    amax1(s)
                if s >= 1:
                    amax2(s - 1)
                if s < B:
                    smooth1(s)
                if s >= 1:
                    smooth2(s - 1)
                    scales2(s - 1)
                if s < B:
                    scales1(s)
                if s >= 1:
                    expert_out(s - 1)
                    stats2(s - 1)
                    norm2(s - 1)
                    choose(s - 1)
                    place(s - 1)
                if s == 0:
                    down_amax()

            def expert_in(e):
                dve.wait_ge(rows_here if e == 0 else rest_here, 16)
                if e >= 2:
                    dve.wait_ge(xT_ready, e - 1)
                nc.vector.tensor_scalar(xg[:, e % 2], gr[:, e, 0:D], gr[:, e, MEAN:MEAN + 1],
                                        gr[:, e, RSTD:RSTD + 1], ALU.subtract, ALU.mult).then_inc(xg_ready, 1)

            def expert_turned(e):
                dve.wait_ge(xT_ready, e + 1)
                if e >= 2:
                    dve.wait_ge(hid_ready, 2 * (e - 1))
                nc.vector.tensor_copy(xgT[:, e % 2].rearrange("p k c -> p (k c)"),
                                      XT[e % 2][:, 0:K * C]).then_inc(xgT_ready, 1)

            expert_in(0)
            expert_turned(0)
            expert_in(1)
            expert_turned(1)
            dve.wait_ge(exp_ready, 1)
            link(nc.vector.tensor_reduce(zs[:], ex[:], AX, ALU.add))
            link(nc.vector.reciprocal(zr[:], zs[:]))
            link(nc.vector.tensor_scalar(gt[:], zr[:], tg[:, 1:2], None, ALU.mult))
            for e in range(E):
                if e + 2 < E:
                    expert_in(e + 2)
                    expert_turned(e + 2)
                dve.wait_ge(y_used, e + 1)
                if e >= 2:
                    dve.wait_ge(out_scattered[e % 2], 16 * (e // 2))
                nc.vector.scalar_tensor_tensor(out=yo[:, e % 2], in0=YB[e % 2][:, 0:D], scalar=gt[:, e:e + 1],
                                               in1=gr[:, e, 0:D], op0=ALU.mult, op1=ALU.add).then_inc(y_ready, 1)

        @block.tensor
        def _(pe):
            pe.wait_ge(consts, 1)

            def turn1(b):
                pe.wait_ge(xn_ready, b + 1)
                pe.wait_ge(cw_here[b], 16)
                if b >= 1:
                    pe.wait_ge(scaled1, b)
                for a, src in ((0, xn), (1, cw[:, b])):
                    for k in range(K):
                        for j in range(J):
                            ins = nc.tensor.transpose(T1[:, a, k * T + j * P:k * T + (j + 1) * P],
                                                      src[:, j, k * P:(k + 1) * P], ident[:])
                ins.then_inc(t1_ready, 1)

            def turn2(b):
                pe.wait_ge(scaled1, b + 1)
                if b >= 1:
                    pe.wait_ge(quant1, b)
                for a in range(2):
                    for j in range(J):
                        for k in range(K):
                            ins = nc.tensor.transpose(T2[:, a, j * D + k * P:j * D + (k + 1) * P],
                                                      xs1[:, a * K + k, j * P:(j + 1) * P], ident[:])
                ins.then_inc(t2_ready, 1)

            def rows1(b):
                pe.wait_ge(recip1_ready, b + 1)
                if b == 1:
                    pe.wait_ge(row1_moved, 1)
                if b >= 2:
                    pe.wait_ge(row2_moved, b - 1)
                for j in range(J):
                    ins = nc.tensor.matmul(R6[:, j * P:(j + 1) * P], q1s[:, b % 2, j:j + 1].to_broadcast([P, P]),
                                           ident[:], start=True, stop=True)
                ins.then_inc(row1_ready, 1)

            def turn3(b):
                pe.wait_ge(rounded1, b + 1)
                if b == 0:
                    pe.wait_ge(consts, 3)
                if b >= 1:
                    pe.wait_ge(up_ready, b)
                t3 = T3.bitcast(BF16)
                for a in range(2):
                    for k in range(K):
                        for j in range(J):
                            o = (a * K + k) * T + j * P
                            ins = nc.tensor.transpose(t3[:, o:o + P], qb1[:, a * J + j, k * P:(k + 1) * P], identb[:])
                ins.then_inc(t3_ready, 1)

            def product1(b):
                pe.wait_ge(moved1, b + 1)
                for h in range(2):
                    for k in range(K):
                        ins = nc.tensor.matmul(T3[:, h * T:(h + 1) * T], qT1[:, K + k, h * P:(h + 1) * P], qT1[:, k, :],
                                               start=(k == 0), stop=(k == K - 1))
                ins.then_inc(h_ready, 1)

            def down_turn():
                pe.wait_ge(dw_here, 16)
                for b in range(B):
                    if b >= 1:
                        pe.wait_ge(dT_moved, b)
                    for k in range(K):
                        ins = nc.tensor.transpose(R7[:, k * P:(k + 1) * P], dw[:, b, k], ident[:])
                    ins.then_inc(dT_ready, 1)

            def turn4(b):
                pe.wait_ge(scaled2, b + 1)
                if b >= 1:
                    pe.wait_ge(y1_ready, b)
                else:
                    pe.wait_ge(dT_moved, B)
                for a in range(2):
                    for j in range(J):
                        c = a * J + j
                        ins = nc.tensor.transpose(R7[:, c * I:(c + 1) * I], aw[:, a, j * P:(j + 1) * P], ident[:])
                ins.then_inc(t4_ready, 1)

            def rows2(b):
                pe.wait_ge(recip2_ready, b + 1)
                if b + 1 < B:
                    pe.wait_ge(row1_moved, b + 2)
                else:
                    pe.wait_ge(row2_moved, b)
                for k in range(K):
                    ins = nc.tensor.matmul(R6[:, k * P:(k + 1) * P], q2s[:, J + k:J + k + 1].to_broadcast([P, P]),
                                           ident[:], start=True, stop=True)
                ins.then_inc(row2_ready, 1)

            def turn5(b):
                pe.wait_ge(rounded2, b + 1)
                t5 = R7.bitcast(BF16)
                for c in range(2 * J):
                    ins = nc.tensor.transpose(t5[:, c * P:(c + 1) * P], qb2[:, c], identb[:])
                ins.then_inc(t5_ready, 1)

            def product2(b):
                pe.wait_ge(moved2, b + 1)
                for j in range(J):
                    ins = nc.tensor.matmul(R7[:, j * D:(j + 1) * D], qT2[:, 0, j * P:(j + 1) * P], qT2[:, 1, :],
                                           start=True, stop=True)
                ins.then_inc(o_ready, 1)

            def turn6(b):
                pe.wait_ge(xn2_ready, b + 1)
                if b >= 1:
                    pe.wait_ge(loc_read, b)
                for k in range(K):
                    for j in range(J):
                        ins = nc.tensor.transpose(R5[:, k * T + j * P:k * T + (j + 1) * P],
                                                  xn2[:, j, k * P:(k + 1) * P], ident[:])
                ins.then_inc(t6_ready, 1)

            def logits(b):
                pe.wait_ge(moved3, b + 1)
                if b == 0:
                    pe.wait_ge(small_here, 48)
                for j in range(J):
                    for k in range(K):
                        ins = nc.tensor.matmul(R5[:, j * E:(j + 1) * E], xn2T[:, k, j * P:(j + 1) * P], wg[:, k],
                                               start=(k == 0), stop=(k == K - 1))
                ins.then_inc(logits_ready, 1)

            def positions(b):
                pe.wait_ge(onehot_ready, b + 1)
                if b == 0:
                    pe.wait_ge(consts, 7)
                for j in range(J):
                    dst = R5[:, 32 + j * E:32 + (j + 1) * E]
                    terms = [(ones, onehot[:, bb, jj]) for bb in range(b) for jj in range(J)]
                    terms += [(upper_eq if jj < j else upper, onehot[:, b, jj]) for jj in range(J)]
                    for n, (tri, hot) in enumerate(terms):
                        ins = nc.tensor.matmul(dst, tri[:], hot, start=(n == 0), stop=(n == len(terms) - 1))
                ins.then_inc(loc_ready, 1)

            for s in range(B + 1):
                if s < B:
                    turn1(s)
                    turn2(s)
                if s >= 1:
                    turn4(s - 1)
                if s < B:
                    rows1(s)
                    turn3(s)
                if s >= 1:
                    rows2(s - 1)
                    turn5(s - 1)
                if s < B:
                    product1(s)
                if s >= 1:
                    product2(s - 1)
                    turn6(s - 1)
                    logits(s - 1)
                    positions(s - 1)
                if s == 0:
                    down_turn()

            def slots_turn(e):
                pe.wait_ge(xg_ready, e + 1)
                if e == 0:
                    pe.wait_ge(loc_read, B)
                if e >= 2:
                    pe.wait_ge(xgT_ready, e - 1)
                xv = xg[:, e % 2].rearrange("p (f k) -> p k f", k=K)
                for k in range(K):
                    ins = nc.tensor.transpose(XT[e % 2][:, k * C:(k + 1) * C], xv[:, k], ident[:])
                ins.then_inc(xT_ready, 1)

            def hidden(e):
                pe.wait_ge(xgT_ready, e + 1)
                pe.wait_ge(w_here[e % NW], 32 * (e // NW + 1))
                wv = w1_sb[:, e % NW].rearrange("p k (f n) -> p k n f", n=NF)
                for m in range(2):
                    if e >= 2:
                        pe.wait_ge(gelu_ready, 2 * (e - 2) + m + 1)
                    for n in range(4):
                        for k in range(K):
                            ins = nc.tensor.matmul(HB[e % 2][:, m, n * C:(n + 1) * C], wv[:, k, 4 * m + n],
                                                   xgT[:, e % 2, k], start=(k == 0), stop=(k == K - 1))
                    ins.then_inc(hid_ready, 1)

            def expert_out(e):
                if e >= 2:
                    pe.wait_ge(y_ready, e - 1)
                for n in range(NF):
                    if n % 4 == 0:
                        pe.wait_ge(gelu_ready, 2 * e + n // 4 + 1)
                    ins = nc.tensor.matmul(YB[e % 2][:, 0:D], hs[:, e % 2, n], w2_sb[:, e % NW, n],
                                           start=(n == 0), stop=(n == NF - 1))
                ins.then_inc(y_used, 1)

            slots_turn(0)
            slots_turn(1)
            hidden(0)
            for e in range(E):
                if e + 2 < E:
                    slots_turn(e + 2)
                if e + 1 < E:
                    hidden(e + 1)
                expert_out(e)


_INS = ['x', 'ctx_gu', 'ctx_d', 'g_xattn', 'g_ffn', 'w_gate', 'w1', 'w2']


def kernel(x, fside_BxS2xS2_0, ctx_1024, g_xattn, g_ffn, L0_ffn_w_gate, L0_ffn_w1, L0_ffn_w2):
    import numpy as _np
    import concourse.bacc as _bacc
    from concourse import mybir as _mybir
    from concourse.bass_utils import run_bass_kernel_spmd as _run

    nc = _bacc.Bacc("TRN2", target_bir_lowering=False, num_devices=1)
    given = [x, fside_BxS2xS2_0, ctx_1024, g_xattn, g_ffn, L0_ffn_w_gate, L0_ffn_w1, L0_ffn_w2]
    arrays, args = {}, []
    for name, a in zip(_INS, given):
        a = _np.ascontiguousarray(a)
        arrays[f"in_{name}"] = a
        args.append(nc.dram_tensor(f"in_{name}", a.shape, _mybir.dt.from_np(a.dtype), kind="ExternalInput").ap())
    tokens = x.shape[0] * x.shape[1]
    scratch = nc.dram_tensor("slot_rows", (tokens, x.shape[2] + 3 + L0_ffn_w_gate.shape[1]), _mybir.dt.float32,
                             kind="Internal").ap()
    out = nc.dram_tensor("out_0", tuple(x.shape), _mybir.dt.float32, kind="ExternalOutput").ap()
    gated_smoothquant_moe_kernel(nc, *args, scratch, out)
    r = _run(nc, [arrays], core_ids=[0])
    return r.results[0]["out_0"]
```

```python
import concourse.bass as bass
from concourse import mybir
from contextlib import ExitStack


def gated_smoothquant_moe_kernel(nc, x_in, ctx_in, down_in, g_xattn, g_ffn, w_gate, w1, w2, scratch, out):
    F32 = mybir.dt.float32
    BF16 = mybir.dt.bfloat16
    I32 = mybir.dt.int32
    ALU = mybir.AluOpType
    ACT = mybir.ActivationFunctionType
    AX = mybir.AxisListType.X

    P = 128
    B, T, D = x_in.shape
    I = down_in.shape[2]
    E, _, F = w1.shape
    J = T // P
    K = D // P
    C = B * T // E
    NF = F // P
    assert (T, D, I, C) == (256, 256, P, P) and ctx_in.shape[1] == 2 * I
    EPS, LN_EPS, QMAX = 1e-6, 1e-5, 127.0
    ROUND = 12582912.0
    DROPPED = 4096.0
    MEAN, RSTD, TOKEN, LOGIT = D, D + 1, D + 2, D + 3
    ROW = LOGIT + E
    NW = 6

    LAG = 2
    TICKS = 41 + LAG * (B - 1)

    ctx = ExitStack()
    with ctx:
        def sb(name, shape, dt=F32):
            return ctx.enter_context(nc.sbuf_tensor(name, shape, dt))

        def ps(name, shape, dt=F32):
            return ctx.enter_context(nc.psum_tensor(name, shape, dt))

        def sem(name):
            return ctx.enter_context(nc.semaphore(name))

        x = sb("x", [P, B, J, D])
        cw = sb("cw", [P, B, J, D])
        dw = sb("dw", [P, B, K, I])
        wg = sb("wg", [P, K, E])
        ident = sb("ident", [P, P])
        identb = sb("identb", [P, P], BF16)
        upper = sb("upper", [P, P], BF16)
        upper_eq = sb("upper_eq", [P, P], BF16)
        ones = sb("ones", [P, P], BF16)
        rank = sb("rank", [P, J, E])
        half = sb("half", [P, K])
        mhalf = sb("mhalf", [P, J])
        rbias = sb("rbias", [P, 1])
        gates = sb("gates", [P, 2])
        tg = sb("tg", [P, 2])
        empty = sb("empty", [P, 1, ROW])
        wide_a = sb("wide_a", [P, B, 2 * K * T])
        wide_b = sb("wide_b", [P, B, 2 * K * T])
        rows_w = sb("rows_w", [P, B, J, D])
        ints = sb("ints", [P, B, 2 * J * D], BF16)
        intsT = sb("intsT", [P, B, 2 * K * T], BF16)
        scrow = sb("scrow", [P, B, T])
        xs1 = wide_a[:].rearrange("p b (c t) -> p b c t", c=2 * K)
        qf1 = wide_b[:].rearrange("p b (c d) -> p b c d", c=2 * J)
        xn = rows_w
        qb1 = ints[:].rearrange("p b (c d) -> p b c d", c=2 * J)
        qT1 = intsT[:].rearrange("p b (c t) -> p b c t", c=2 * K)
        xrow = scrow
        st1 = sb("st1", [P, B, J, 6])
        mv1 = sb("mv1", [P, B, J, 2])
        ve1 = sb("ve1", [P, B, J])
        rs1 = sb("rs1", [P, B, J])
        am1 = sb("am1", [P, B, 2 * K])
        rw1 = sb("rw1", [P, B, K])
        ra1 = sb("ra1", [P, B, K])
        root1 = sb("root1", [P, B, K])
        sc1 = sb("sc1", [P, B, 2 * K])
        am2 = sb("am2", [P, B, 2 * J])
        q1s = sb("q1s", [P, B, 2 * J])
        q1r = sb("q1r", [P, B, 2 * J])
        g_sb = wide_a[:, :, 0:T]
        u_sb = wide_a[:, :, T:2 * T]
        sg = wide_a[:, :, 2 * T:3 * T]
        a_sb = wide_a[:, :, 3 * T:4 * T]
        aw = wide_b[:, :, 0:2 * T].rearrange("p b (c t) -> p b c t", c=2)
        qf2 = wide_b[:, :, 2 * T:4 * T].rearrange("p b (c i) -> p b c i", c=2 * J)
        qb2 = ints[:, :, 0:2 * J * I].rearrange("p b (c i) -> p b c i", c=2 * J)
        qT2 = intsT[:, :, 0:2 * T].rearrange("p b (c t) -> p b c t", c=2)
        drow = scrow
        y1 = rows_w
        amd = sb("amd", [P, B])
        rwd = sb("rwd", [P, B])
        ama = sb("ama", [P, B])
        ra2 = sb("ra2", [P, B])
        root2 = sb("root2", [P, B])
        sc3 = sb("sc3", [P, B, 2])
        am4 = sb("am4", [P, B, 2 * J])
        q2s = sb("q2s", [P, B, 2 * J])
        q2r = sb("q2r", [P, B, 2 * J])
        q2g = sb("q2g", [P, B, J])
        row = sb("row", [P, B, J, ROW])
        st2 = sb("st2", [P, B, J, 6])
        mv2 = sb("mv2", [P, B, J, 2])
        ve2 = sb("ve2", [P, B, J])
        xn2 = rows_w
        xn2T = wide_b[:, :, 0:K * T].rearrange("p b (k t) -> p b k t", k=K)
        lmax = sb("lmax", [P, B, J])
        prio = sb("prio", [P, B, J, E])
        pmax = sb("pmax", [P, B, J])
        base = sb("base", [P, B, J])
        onehot = sb("onehot", [P, B, J, E], BF16)
        locm = sb("locm", [P, B, J, E])
        loc = sb("loc", [P, B, J])
        over = sb("over", [P, B, J])
        where_ = sb("where_", [P, B, J])
        slot = sb("slot", [P, B, J], I32)
        w1_sb = sb("w1_sb", [P, NW, K, F])
        w2_sb = sb("w2_sb", [P, NW, NF, D])
        gr = sb("gr", [P, E, ROW])
        ex = sb("ex", [P, E, E])
        zs = sb("zs", [P, E])
        zr = sb("zr", [P, E])
        gt = sb("gt", [P, E])
        xg = sb("xg", [P, 2, D])
        xgT = sb("xgT", [P, 2, K, C])
        hs = wide_a[:, 0:2].rearrange("p a (n c) -> p a n c", c=C)
        yo = sb("yo", [P, 2, D])

        bk = [ps(f"bk{i}", [P, 2, 512]) for i in range(B)]
        HB = [bk[0], bk[1]]
        XT = [bk[2][:, 0, :], bk[2][:, 1, :]]
        YB = [bk[3][:, 0, :], bk[3][:, 1, :]]

        x_here = [sem(f"x_here{b}") for b in range(B)]
        cw_here = [sem(f"cw_here{b}") for b in range(B)]
        small_here = sem("small_here")
        dw_here = sem("dw_here")
        scratch_clear = sem("scratch_clear")
        w_here = [sem(f"w_here{i}") for i in range(NW)]
        plain_out = sem("plain_out")
        rows_scattered = sem("rows_scattered")
        rows_here = sem("rows_here")
        rest_here = sem("rest_here")
        out_scattered = [sem("out_scattered0"), sem("out_scattered1")]
        consts = sem("consts")
        pool_c = sem("pool_c")
        dve_c = sem("dve_c")
        dve_consts = sem("dve_consts")
        tanh_ready = sem("tanh_ready")
        var1_ready, rstd1_ready, xn_ready = sem("var1_ready"), sem("rstd1_ready"), sem("xn_ready")
        t1_ready, ratio1_ready, root1_ready = sem("t1_ready"), sem("ratio1_ready"), sem("root1_ready")
        scale1_ready, scaled1, t2_ready = sem("scale1_ready"), sem("scaled1"), sem("t2_ready")
        recip1_ready, quant1, rounded1 = sem("recip1_ready"), sem("quant1"), sem("rounded1")
        t3_ready, moved1, row1_ready, row1_moved = sem("t3_ready"), sem("moved1"), sem("row1_ready"), sem("row1_moved")
        h_ready, gate_ready, up_ready = sem("h_ready"), sem("gate_ready"), sem("up_ready")
        silu_ready, act_ready = sem("silu_ready"), sem("act_ready")
        dT_ready, damax_ready = sem("dT_ready"), sem("damax_ready")
        ratio2_ready, root2_ready, scale2_ready = sem("ratio2_ready"), sem("root2_ready"), sem("scale2_ready")
        scaled2, t4_ready, recip2_ready = sem("scaled2"), sem("t4_ready"), sem("recip2_ready")
        quant2, rounded2, t5_ready, moved2 = sem("quant2"), sem("rounded2"), sem("t5_ready"), sem("moved2")
        row2_ready, row2_moved, o_ready, y1_ready = sem("row2_ready"), sem("row2_moved"), sem("o_ready"), sem("y1_ready")
        x1_ready, var2_ready, rstd2_ready, xn2_ready = sem("x1_ready"), sem("var2_ready"), sem("rstd2_ready"), sem("xn2_ready")
        t6_ready, moved3, logits_ready = sem("t6_ready"), sem("moved3"), sem("logits_ready")
        onehot_ready, loc_ready, slot_ready = sem("onehot_ready"), sem("loc_ready"), sem("slot_ready")
        exp_ready, gt_ready = sem("exp_ready"), sem("gt_ready")
        xg_ready, xT_ready, xgT_ready = sem("xg_ready"), sem("xT_ready"), sem("xgT_ready")
        hid_ready, gelu_ready, y_ready, y_used = sem("hid_ready"), sem("gelu_ready"), sem("y_ready"), sem("y_used")

        block = ctx.enter_context(nc.Block())

        @block.sync
        def _(sp):
            for b in range(B):
                sp.dma_start(x[:, b], x_in[b].rearrange("(p j) d -> p j d", j=J)).then_inc(x_here[b], 16)
                sp.dma_start(cw[:, b], ctx_in[b].rearrange("(j p) d -> p j d", p=P)).then_inc(cw_here[b], 16)
                if b == 0:
                    sp.dma_start(dw[:], down_in.rearrange("b (k p) i -> p b k i", p=P)).then_inc(dw_here, 16)
                    sp.dma_start(gates[:, 0:1], g_xattn.partition_broadcast(P)).then_inc(small_here, 16)
                    sp.dma_start(gates[:, 1:2], g_ffn.partition_broadcast(P)).then_inc(small_here, 16)
                    sp.dma_start(wg[:], w_gate.rearrange("(k p) e -> p k e", p=P)).then_inc(small_here, 16)
            sp.wait_ge(consts, 2)
            sp.dma_start(scratch.rearrange("(e p) r -> p e r", p=P), empty[:].to_broadcast([P, E, ROW])).then_inc(scratch_clear, 16)

            def load(e):
                if e >= 1:
                    sp.wait_ge(w_here[(e - 1) % NW], 32 * ((e - 1) // NW + 1))
                if e >= NW:
                    sp.wait_ge(y_ready, e - NW + 1)
                sp.dma_start(w1_sb[:, e % NW], w1[e].rearrange("(p k) f -> p k f", k=K)).then_inc(w_here[e % NW], 16)
                sp.dma_start(w2_sb[:, e % NW], w2[e].rearrange("(p n) d -> p n d", n=NF)).then_inc(w_here[e % NW], 16)

            for e in range(NW):
                load(e)
            for b in range(B):
                sp.wait_ge(x1_ready, b + 1)
                sp.dma_start(out[b].rearrange("(p j) d -> p j d", j=J), row[:, b, :, 0:D]).then_inc(plain_out, 16)
            for e in range(NW, E):
                load(e)
            for n in range(2):
                sp.wait_ge(out_scattered[n], 16 * (E // 2))

        @block.gpsimd
        def _(pool):
            nc.gpsimd.memset(ident[:], 0.0).then_inc(pool_c, 1)
            nc.gpsimd.memset(upper[:], 1.0).then_inc(pool_c, 1)
            nc.gpsimd.memset(upper_eq[:], 1.0).then_inc(pool_c, 1)
            nc.gpsimd.memset(empty[:], 0.0).then_inc(pool_c, 1)
            nc.gpsimd.memset(identb[:], 0.0).then_inc(pool_c, 1)
            pool.wait_ge(pool_c, 5)
            nc.gpsimd.affine_select(out=ident[:], in_=ident[:], compare_op=ALU.not_equal, fill=1.0, base=0,
                                    pattern=[[-1, P]], channel_multiplier=1).then_inc(consts, 1)
            nc.gpsimd.iota(empty[:, :, TOKEN:TOKEN + 1].bitcast(I32), pattern=[[0, 1]], base=1 << 20,
                           channel_multiplier=0).then_inc(consts, 1)
            nc.gpsimd.affine_select(out=identb[:], in_=identb[:], compare_op=ALU.not_equal, fill=1.0, base=0,
                                    pattern=[[-1, P]], channel_multiplier=1).then_inc(consts, 1)
            nc.gpsimd.affine_select(out=upper[:], in_=upper[:], compare_op=ALU.is_gt, fill=0.0, base=0,
                                    pattern=[[1, P]], channel_multiplier=-1).then_inc(consts, 1)
            nc.gpsimd.affine_select(out=upper_eq[:], in_=upper_eq[:], compare_op=ALU.is_ge, fill=0.0, base=0,
                                    pattern=[[1, P]], channel_multiplier=-1).then_inc(consts, 1)
            nc.gpsimd.iota(rank[:], pattern=[[0, J], [-1, E]], base=E, channel_multiplier=0,
                           allow_small_or_imprecise_dtypes=True).then_inc(consts, 1)
            nc.gpsimd.iota(row[:, :, :, TOKEN:TOKEN + 1].bitcast(I32), pattern=[[T, B], [1, J]], base=0,
                           channel_multiplier=J).then_inc(consts, 1)

            def rstd1(b):
                pool.wait_ge(var1_ready, b + 1)
                nc.gpsimd.tensor_tensor(rs1[:, b], ve1[:, b], mhalf[:], ALU.pow).then_inc(rstd1_ready, 1)

            def root_1(b):
                pool.wait_ge(ratio1_ready, b + 1)
                nc.gpsimd.tensor_tensor(root1[:, b], ra1[:, b], half[:], ALU.pow).then_inc(root1_ready, 1)

            def round1(b):
                pool.wait_ge(quant1, b + 1)
                nc.gpsimd.tensor_scalar(qb1[:, b], qf1[:, b], -ROUND, 1.0, ALU.add, ALU.mult).then_inc(rounded1, 1)

            def act_product(b):
                pool.wait_ge(silu_ready, b + 1)
                pool.wait_ge(up_ready, b + 1)
                nc.gpsimd.tensor_tensor(a_sb[:, b], sg[:, b], u_sb[:, b], ALU.mult).then_inc(act_ready, 1)

            def root_2(b):
                pool.wait_ge(ratio2_ready, b + 1)
                nc.gpsimd.tensor_tensor(root2[:, b:b + 1], ra2[:, b:b + 1], half[:, 0:1],
                                        ALU.pow).then_inc(root2_ready, 1)

            def round2(b):
                pool.wait_ge(quant2, b + 1)
                nc.gpsimd.tensor_scalar(qb2[:, b], qf2[:, b], -ROUND, 1.0, ALU.add, ALU.mult).then_inc(rounded2, 1)

            def residual(b):
                pool.wait_ge(y1_ready, b + 1)
                nc.gpsimd.tensor_tensor(row[:, b, :, 0:D], x[:, b], y1[:, b], ALU.add).then_inc(x1_ready, 1)

            def rstd2(b):
                pool.wait_ge(var2_ready, b + 1)
                nc.gpsimd.tensor_tensor(row[:, b, :, RSTD], ve2[:, b], mhalf[:], ALU.pow).then_inc(rstd2_ready, 1)

            def scatter(b):
                pool.wait_ge(slot_ready, b + 1)
                if b == 0:
                    pool.wait_ge(scratch_clear, 16)
                    pool.wait_ge(consts, 7)
                for j in range(J):
                    nc.gpsimd.indirect_dma_start(
                        scratch, bass.IndirectOffsetOnAxis(ap=slot[:, b, j:j + 1], axis=0), row[:, b, j, :], None,
                        bounds_check=E * C - 1, oob_is_err=False).then_inc(rows_scattered, 16)

            pool.wait_ge(dve_consts, 1)
            for t in range(TICKS):
                for b in range(B):
                    k = t - LAG * b
                    if k == 1:
                        rstd1(b)
                    if k == 5:
                        root_1(b)
                    if k == 11:
                        round1(b)
                    if k == 17:
                        act_product(b)
                    if k == 19:
                        root_2(b)
                    if k == 25:
                        round2(b)
                    if k == 30:
                        residual(b)
                    if k == 32:
                        rstd2(b)
                    if k == 40:
                        scatter(b)

            out_rows = out.rearrange("b t d -> (b t) d")
            for e in range(E):
                pool.wait_ge(y_ready, e + 1)
                if e == 0:
                    pool.wait_ge(plain_out, 16 * B)
                nc.gpsimd.indirect_dma_start(
                    out_rows, bass.IndirectOffsetOnAxis(ap=gr[:, e, TOKEN:TOKEN + 1].bitcast(I32), axis=0),
                    yo[:, e % 2, :], None, bounds_check=B * T - 1, oob_is_err=False).then_inc(out_scattered[e % 2], 16)

        @block.scalar
        def _(act):
            act.wait_ge(small_here, 48)
            nc.scalar.activation(tg[:], gates[:], ACT.Tanh).then_inc(tanh_ready, 1)
            act.wait_ge(dve_consts, 1)

            def scale1(b):
                act.wait_ge(scale1_ready, b + 1)
                for c in range(2 * K):
                    last = nc.scalar.activation(xs1[:, b, c], bk[b][:, c // K, (c % K) * T:(c % K + 1) * T],
                                                ACT.Identity, scale=sc1[:, b, c:c + 1])
                last.then_inc(scaled1, 1)

            def quantise1(b):
                act.wait_ge(recip1_ready, b + 1)
                for c in range(2 * J):
                    last = nc.scalar.activation(qf1[:, b, c], bk[b][:, c // J, (c % J) * D:(c % J + 1) * D],
                                                ACT.Identity, scale=q1r[:, b, c:c + 1], bias=rbias[:, 0:1])
                last.then_inc(quant1, 1)

            def move_row1(b):
                act.wait_ge(row1_ready, b + 1)
                nc.scalar.activation(xrow[:, b], bk[b][:, 1, 0:T], ACT.Copy).then_inc(row1_moved, 1)

            def move1(b):
                act.wait_ge(t3_ready, b + 1)
                nc.scalar.activation(intsT[:, b].bitcast(F32), bk[b][:, 0, :], ACT.Copy).then_inc(moved1, 1)

            def silu(b):
                act.wait_ge(gate_ready, b + 1)
                nc.scalar.activation(sg[:, b], g_sb[:, b], ACT.Silu).then_inc(silu_ready, 1)

            def scale2(b):
                act.wait_ge(scale2_ready, b + 1)
                nc.scalar.activation(aw[:, b, 0], a_sb[:, b], ACT.Identity, scale=sc3[:, b, 0:1])
                nc.scalar.activation(aw[:, b, 1], bk[b][:, 1, 0:D], ACT.Identity,
                                     scale=sc3[:, b, 1:2]).then_inc(scaled2, 1)

            def quantise2(b):
                act.wait_ge(recip2_ready, b + 1)
                for c in range(2 * J):
                    last = nc.scalar.activation(qf2[:, b, c], bk[b][:, 0, c * I:(c + 1) * I], ACT.Identity,
                                                scale=q2r[:, b, c:c + 1], bias=rbias[:, 0:1])
                last.then_inc(quant2, 1)

            def move_row2(b):
                act.wait_ge(row2_ready, b + 1)
                nc.scalar.activation(drow[:, b], bk[b][:, 1, 0:D], ACT.Copy).then_inc(row2_moved, 1)

            def move2(b):
                act.wait_ge(t5_ready, b + 1)
                nc.scalar.activation(intsT[:, b, 0:2 * T].bitcast(F32), bk[b][:, 0, 0:T],
                                     ACT.Copy).then_inc(moved2, 1)

            def move3(b):
                act.wait_ge(t6_ready, b + 1)
                nc.scalar.activation(wide_b[:, b, 0:K * T], bk[b][:, 0, :], ACT.Copy).then_inc(moved3, 1)

            for t in range(TICKS):
                for b in range(B):
                    k = t - LAG * b
                    if k == 7:
                        scale1(b)
                    if k == 10:
                        quantise1(b)
                    if k == 11:
                        move_row1(b)
                    if k == 13:
                        move1(b)
                    if k == 16:
                        silu(b)
                    if k == 21:
                        scale2(b)
                    if k == 24:
                        quantise2(b)
                    if k == 25:
                        move_row2(b)
                    if k == 27:
                        move2(b)
                    if k == 35:
                        move3(b)

            sc_rows = scratch.rearrange("(e p) r -> p e r", p=P)
            act.wait_ge(rows_scattered, 16 * B * J)
            act.dma_start(gr[:, 0:1], sc_rows[:, 0:1]).then_inc(rows_here, 16)
            act.dma_start(gr[:, 1:E], sc_rows[:, 1:E]).then_inc(rest_here, 16)
            act.wait_ge(rows_here, 16)
            act.wait_ge(rest_here, 16)
            nc.scalar.activation(ex[:], gr[:, :, LOGIT:ROW], ACT.Exp).then_inc(exp_ready, 1)
            for e in range(E):
                for m in range(2):
                    act.wait_ge(hid_ready, 2 * e + m + 1)
                    if e >= 2:
                        act.wait_ge(y_used, e - 1)
                    nc.scalar.activation(hs[:, e % 2, 4 * m:4 * m + 4].rearrange("p n c -> p (n c)"),
                                         HB[e % 2][:, m, :], ACT.Gelu_apprx_tanh).then_inc(gelu_ready, 1)

        @block.vector
        def _(dve):
            chain = [0]

            def link(ins):
                chain[0] += 1
                ins.then_inc(dve_c, 1)
                dve.wait_ge(dve_c, chain[0])

            nc.vector.memset(half[:], 0.5)
            nc.vector.memset(mhalf[:], -0.5)
            nc.vector.memset(ones[:], 1.0)
            nc.vector.memset(rbias[:], ROUND).then_inc(dve_consts, 1)

            def stats1(b):
                dve.wait_ge(x_here[b], 16)
                for j in range(J):
                    ins = nc.vector.bn_stats(st1[:, b, j], x[:, b, j])
                link(ins)
                for j in range(J):
                    ins = nc.vector.bn_aggr(mv1[:, b, j], st1[:, b, j])
                link(ins)
                nc.vector.tensor_scalar(ve1[:, b], mv1[:, b, :, 1], LN_EPS, None, ALU.add).then_inc(var1_ready, 1)

            def norm1(b):
                dve.wait_ge(rstd1_ready, b + 1)
                for j in range(J):
                    ins = nc.vector.tensor_scalar(xn[:, b, j], x[:, b, j], mv1[:, b, j, 0:1], rs1[:, b, j:j + 1],
                                                  ALU.subtract, ALU.mult)
                ins.then_inc(xn_ready, 1)

            def amax1(b):
                dve.wait_ge(t1_ready, b + 1)
                link(nc.vector.tensor_reduce(am1[:, b], bk[b][:].rearrange("p a (k t) -> p (a k) t", k=K), AX, ALU.max,
                                             apply_absolute_value=True))
                link(nc.vector.tensor_scalar(am1[:, b], am1[:, b], EPS, None, ALU.max))
                link(nc.vector.reciprocal(rw1[:, b], am1[:, b, K:2 * K]))
                nc.vector.tensor_tensor(ra1[:, b], am1[:, b, 0:K], rw1[:, b], ALU.mult).then_inc(ratio1_ready, 1)

            def smooth1(b):
                dve.wait_ge(root1_ready, b + 1)
                link(nc.vector.tensor_scalar(sc1[:, b, K:2 * K], root1[:, b], EPS, None, ALU.max))
                nc.vector.reciprocal(sc1[:, b, 0:K], sc1[:, b, K:2 * K]).then_inc(scale1_ready, 1)

            def scales1(b):
                dve.wait_ge(t2_ready, b + 1)
                link(nc.vector.tensor_reduce(am2[:, b], bk[b][:].rearrange("p a (j d) -> p (a j) d", j=J), AX, ALU.max,
                                             apply_absolute_value=True))
                link(nc.vector.tensor_scalar(q1s[:, b], am2[:, b], EPS, 1.0 / QMAX, ALU.max, ALU.mult))
                nc.vector.reciprocal(q1r[:, b], q1s[:, b]).then_inc(recip1_ready, 1)

            def gate_up(b):
                dve.wait_ge(h_ready, b + 1)
                dve.wait_ge(row1_moved, b + 1)
                for h, (dst, done) in enumerate(((g_sb, gate_ready), (u_sb, up_ready))):
                    nc.vector.scalar_tensor_tensor(out=dst[:, b], in0=bk[b][:, 0, h * T:(h + 1) * T],
                                                   scalar=q1s[:, b, J + h:J + h + 1], in1=xrow[:, b],
                                                   op0=ALU.mult, op1=ALU.mult).then_inc(done, 1)

            def down_amax(b):
                dve.wait_ge(dT_ready, b + 1)
                link(nc.vector.tensor_reduce(amd[:, b:b + 1], bk[b][:, 1, 0:D], AX, ALU.max, apply_absolute_value=True))
                link(nc.vector.tensor_scalar(amd[:, b:b + 1], amd[:, b:b + 1], EPS, None, ALU.max))
                link(nc.vector.reciprocal(rwd[:, b:b + 1], amd[:, b:b + 1]))

            def amax2(b):
                dve.wait_ge(act_ready, b + 1)
                link(nc.vector.tensor_reduce(ama[:, b:b + 1], a_sb[:, b], AX, ALU.max, apply_absolute_value=True))
                nc.vector.tensor_scalar(ra2[:, b:b + 1], ama[:, b:b + 1], EPS, rwd[:, b:b + 1], ALU.max,
                                        ALU.mult).then_inc(ratio2_ready, 1)

            def smooth2(b):
                dve.wait_ge(root2_ready, b + 1)
                link(nc.vector.tensor_scalar(sc3[:, b, 1:2], root2[:, b:b + 1], EPS, None, ALU.max))
                nc.vector.reciprocal(sc3[:, b, 0:1], sc3[:, b, 1:2]).then_inc(scale2_ready, 1)

            def scales2(b):
                dve.wait_ge(t4_ready, b + 1)
                link(nc.vector.tensor_reduce(am4[:, b], bk[b][:, 0, :].rearrange("p (c i) -> p c i", i=I), AX, ALU.max,
                                             apply_absolute_value=True))
                link(nc.vector.tensor_scalar(q2s[:, b], am4[:, b], EPS, 1.0 / QMAX, ALU.max, ALU.mult))
                nc.vector.reciprocal(q2r[:, b], q2s[:, b]).then_inc(recip2_ready, 1)
                if b == 0:
                    dve.wait_ge(tanh_ready, 1)
                link(nc.vector.tensor_scalar(q2g[:, b], q2s[:, b, 0:J], tg[:, 0:1], None, ALU.mult))

            def expert_out(b):
                dve.wait_ge(o_ready, b + 1)
                dve.wait_ge(row2_moved, b + 1)
                for j in range(J):
                    ins = nc.vector.scalar_tensor_tensor(out=y1[:, b, j], in0=bk[b][:, 0, j * D:(j + 1) * D],
                                                         scalar=q2g[:, b, j:j + 1], in1=drow[:, b],
                                                         op0=ALU.mult, op1=ALU.mult)
                ins.then_inc(y1_ready, 1)

            def stats2(b):
                dve.wait_ge(x1_ready, b + 1)
                for j in range(J):
                    ins = nc.vector.bn_stats(st2[:, b, j], row[:, b, j, 0:D])
                link(ins)
                for j in range(J):
                    ins = nc.vector.bn_aggr(mv2[:, b, j], st2[:, b, j])
                link(ins)
                nc.vector.tensor_scalar(ve2[:, b], mv2[:, b, :, 1], LN_EPS, None, ALU.add).then_inc(var2_ready, 1)
                link(nc.vector.tensor_copy(row[:, b, :, MEAN], mv2[:, b, :, 0]))

            def norm2(b):
                dve.wait_ge(rstd2_ready, b + 1)
                for j in range(J):
                    ins = nc.vector.tensor_scalar(xn2[:, b, j], row[:, b, j, 0:D], row[:, b, j, MEAN:MEAN + 1],
                                                  row[:, b, j, RSTD:RSTD + 1], ALU.subtract, ALU.mult)
                ins.then_inc(xn2_ready, 1)

            def choose(b):
                dve.wait_ge(logits_ready, b + 1)
                if b == 0:
                    dve.wait_ge(consts, 7)
                lg = bk[b][:, 1, 0:J * E].rearrange("p (j e) -> p j e", e=E)
                link(nc.vector.tensor_reduce(lmax[:, b], lg, AX, ALU.max))
                lrel = row[:, b, :, LOGIT:ROW]
                link(nc.vector.tensor_tensor(lrel, lg, lmax[:, b].unsqueeze(2).to_broadcast([P, J, E]), ALU.subtract))
                link(nc.vector.scalar_tensor_tensor(out=prio[:, b], in0=lrel, scalar=0.0, in1=rank[:],
                                                    op0=ALU.is_ge, op1=ALU.mult))
                link(nc.vector.tensor_reduce(pmax[:, b], prio[:, b], AX, ALU.max))
                nc.vector.tensor_tensor(onehot[:, b], prio[:, b], pmax[:, b].unsqueeze(2).to_broadcast([P, J, E]),
                                        ALU.is_equal).then_inc(onehot_ready, 1)
                nc.vector.tensor_scalar(base[:, b], pmax[:, b], -float(C), float(C * E), ALU.mult, ALU.add)

            def place(b):
                dve.wait_ge(loc_ready, b + 1)
                dve.wait_ge(onehot_ready, b + 1)
                link(nc.vector.tensor_tensor(locm[:, b], bk[b][:, 1, J * E:2 * J * E].rearrange("p (j e) -> p j e", e=E),
                                             onehot[:, b], ALU.mult))
                link(nc.vector.tensor_reduce(loc[:, b], locm[:, b], AX, ALU.add))
                nc.vector.tensor_scalar(over[:, b], loc[:, b], float(C), DROPPED, ALU.is_ge, ALU.mult)
                link(nc.vector.tensor_tensor(where_[:, b], loc[:, b], base[:, b], ALU.add))
                nc.vector.tensor_tensor(slot[:, b], where_[:, b], over[:, b], ALU.add).then_inc(slot_ready, 1)

            for t in range(TICKS):
                for b in range(B):
                    k = t - LAG * b
                    if k == 0:
                        stats1(b)
                    if k == 2:
                        norm1(b)
                    if k == 4:
                        amax1(b)
                    if k == 6:
                        smooth1(b)
                    if k == 9:
                        scales1(b)
                    if k == 15:
                        gate_up(b)
                    if k == 16:
                        down_amax(b)
                    if k == 18:
                        amax2(b)
                    if k == 20:
                        smooth2(b)
                    if k == 23:
                        scales2(b)
                    if k == 29:
                        expert_out(b)
                    if k == 31:
                        stats2(b)
                    if k == 33:
                        norm2(b)
                    if k == 37:
                        choose(b)
                    if k == 39:
                        place(b)

            def expert_in(e):
                dve.wait_ge(rows_here if e == 0 else rest_here, 16)
                if e >= 2:
                    dve.wait_ge(xT_ready, e - 1)
                nc.vector.tensor_scalar(xg[:, e % 2], gr[:, e, 0:D], gr[:, e, MEAN:MEAN + 1],
                                        gr[:, e, RSTD:RSTD + 1], ALU.subtract, ALU.mult).then_inc(xg_ready, 1)

            def expert_turned(e):
                dve.wait_ge(xT_ready, e + 1)
                if e >= 2:
                    dve.wait_ge(hid_ready, 2 * (e - 1))
                nc.vector.tensor_copy(xgT[:, e % 2].rearrange("p k c -> p (k c)"),
                                      XT[e % 2][:, 0:K * C]).then_inc(xgT_ready, 1)

            expert_in(0)
            expert_turned(0)
            expert_in(1)
            expert_turned(1)
            dve.wait_ge(exp_ready, 1)
            link(nc.vector.tensor_reduce(zs[:], ex[:], AX, ALU.add))
            link(nc.vector.reciprocal(zr[:], zs[:]))
            link(nc.vector.tensor_scalar(gt[:], zr[:], tg[:, 1:2], None, ALU.mult))
            for e in range(E):
                if e + 2 < E:
                    expert_in(e + 2)
                    expert_turned(e + 2)
                dve.wait_ge(y_used, e + 1)
                if e >= 2:
                    dve.wait_ge(out_scattered[e % 2], 16 * (e // 2))
                nc.vector.scalar_tensor_tensor(out=yo[:, e % 2], in0=YB[e % 2][:, 0:D], scalar=gt[:, e:e + 1],
                                               in1=gr[:, e, 0:D], op0=ALU.mult, op1=ALU.add).then_inc(y_ready, 1)

        @block.tensor
        def _(pe):
            pe.wait_ge(consts, 1)

            def turn1(b):
                pe.wait_ge(cw_here[b], 16)
                for a, src in ((1, cw), (0, xn)):
                    if a == 0:
                        pe.wait_ge(xn_ready, b + 1)
                    for k in range(K):
                        for j in range(J):
                            ins = nc.tensor.transpose(bk[b][:, a, k * T + j * P:k * T + (j + 1) * P],
                                                      src[:, b, j, k * P:(k + 1) * P], ident[:])
                ins.then_inc(t1_ready, 1)

            def turn2(b):
                pe.wait_ge(scaled1, b + 1)
                for a in range(2):
                    for j in range(J):
                        for k in range(K):
                            ins = nc.tensor.transpose(bk[b][:, a, j * D + k * P:j * D + (k + 1) * P],
                                                      xs1[:, b, a * K + k, j * P:(j + 1) * P], ident[:])
                ins.then_inc(t2_ready, 1)

            def rows1(b):
                pe.wait_ge(quant1, b + 1)
                for j in range(J):
                    ins = nc.tensor.matmul(bk[b][:, 1, j * P:(j + 1) * P], q1s[:, b, j:j + 1].to_broadcast([P, P]),
                                           ident[:], start=True, stop=True)
                ins.then_inc(row1_ready, 1)

            def turn3(b):
                pe.wait_ge(rounded1, b + 1)
                if b == 0:
                    pe.wait_ge(consts, 3)
                t3 = bk[b][:, 0, :].bitcast(BF16)
                for a in range(2):
                    for k in range(K):
                        for j in range(J):
                            o = (a * K + k) * T + j * P
                            ins = nc.tensor.transpose(t3[:, o:o + P], qb1[:, b, a * J + j, k * P:(k + 1) * P],
                                                      identb[:])
                ins.then_inc(t3_ready, 1)

            def product1(b):
                pe.wait_ge(moved1, b + 1)
                for h in range(2):
                    for k in range(K):
                        ins = nc.tensor.matmul(bk[b][:, 0, h * T:(h + 1) * T], qT1[:, b, K + k, h * P:(h + 1) * P],
                                               qT1[:, b, k, :], start=(k == 0), stop=(k == K - 1))
                ins.then_inc(h_ready, 1)

            def down_turn(b):
                pe.wait_ge(dw_here, 16)
                pe.wait_ge(row1_moved, b + 1)
                for k in range(K):
                    ins = nc.tensor.transpose(bk[b][:, 1, k * P:(k + 1) * P], dw[:, b, k], ident[:])
                ins.then_inc(dT_ready, 1)

            def turn4(b):
                pe.wait_ge(scaled2, b + 1)
                for a in range(2):
                    for j in range(J):
                        c = a * J + j
                        ins = nc.tensor.transpose(bk[b][:, 0, c * I:(c + 1) * I], aw[:, b, a, j * P:(j + 1) * P],
                                                  ident[:])
                ins.then_inc(t4_ready, 1)

            def rows2(b):
                pe.wait_ge(recip2_ready, b + 1)
                for k in range(K):
                    ins = nc.tensor.matmul(bk[b][:, 1, k * P:(k + 1) * P],
                                           q2s[:, b, J + k:J + k + 1].to_broadcast([P, P]),
                                           ident[:], start=True, stop=True)
                ins.then_inc(row2_ready, 1)

            def turn5(b):
                pe.wait_ge(rounded2, b + 1)
                t5 = bk[b][:, 0, :].bitcast(BF16)
                for c in range(2 * J):
                    ins = nc.tensor.transpose(t5[:, c * P:(c + 1) * P], qb2[:, b, c], identb[:])
                ins.then_inc(t5_ready, 1)

            def product2(b):
                pe.wait_ge(moved2, b + 1)
                for j in range(J):
                    ins = nc.tensor.matmul(bk[b][:, 0, j * D:(j + 1) * D], qT2[:, b, 0, j * P:(j + 1) * P],
                                           qT2[:, b, 1, :], start=True, stop=True)
                ins.then_inc(o_ready, 1)

            def turn6(b):
                pe.wait_ge(xn2_ready, b + 1)
                for k in range(K):
                    for j in range(J):
                        ins = nc.tensor.transpose(bk[b][:, 0, k * T + j * P:k * T + (j + 1) * P],
                                                  xn2[:, b, j, k * P:(k + 1) * P], ident[:])
                ins.then_inc(t6_ready, 1)

            def logits(b):
                pe.wait_ge(moved3, b + 1)
                if b == 0:
                    pe.wait_ge(small_here, 48)
                for j in range(J):
                    for k in range(K):
                        ins = nc.tensor.matmul(bk[b][:, 1, j * E:(j + 1) * E], xn2T[:, b, k, j * P:(j + 1) * P],
                                               wg[:, k], start=(k == 0), stop=(k == K - 1))
                ins.then_inc(logits_ready, 1)

            def positions(b):
                pe.wait_ge(onehot_ready, b + 1)
                if b == 0:
                    pe.wait_ge(consts, 7)
                for j in range(J):
                    dst = bk[b][:, 1, (J + j) * E:(J + j + 1) * E]
                    terms = [(ones, onehot[:, bb, jj]) for bb in range(b) for jj in range(J)]
                    terms += [(upper_eq if jj < j else upper, onehot[:, b, jj]) for jj in range(J)]
                    for n, (tri, hot) in enumerate(terms):
                        ins = nc.tensor.matmul(dst, tri[:], hot, start=(n == 0), stop=(n == len(terms) - 1))
                ins.then_inc(loc_ready, 1)

            for t in range(TICKS):
                for b in range(B):
                    k = t - LAG * b
                    if k == 3:
                        turn1(b)
                    if k == 8:
                        turn2(b)
                    if k == 10:
                        rows1(b)
                    if k == 12:
                        turn3(b)
                    if k == 14:
                        product1(b)
                        down_turn(b)
                    if k == 22:
                        turn4(b)
                    if k == 24:
                        rows2(b)
                    if k == 26:
                        turn5(b)
                    if k == 28:
                        product2(b)
                    if k == 34:
                        turn6(b)
                    if k == 36:
                        logits(b)
                    if k == 38:
                        positions(b)

            def slots_turn(e):
                pe.wait_ge(xg_ready, e + 1)
                if e == 0:
                    pe.wait_ge(slot_ready, B)
                if e >= 2:
                    pe.wait_ge(xgT_ready, e - 1)
                xv = xg[:, e % 2].rearrange("p (f k) -> p k f", k=K)
                for k in range(K):
                    ins = nc.tensor.transpose(XT[e % 2][:, k * C:(k + 1) * C], xv[:, k], ident[:])
                ins.then_inc(xT_ready, 1)

            def hidden(e):
                pe.wait_ge(xgT_ready, e + 1)
                pe.wait_ge(w_here[e % NW], 32 * (e // NW + 1))
                wv = w1_sb[:, e % NW].rearrange("p k (f n) -> p k n f", n=NF)
                for m in range(2):
                    if e >= 2:
                        pe.wait_ge(gelu_ready, 2 * (e - 2) + m + 1)
                    for n in range(4):
                        for k in range(K):
                            ins = nc.tensor.matmul(HB[e % 2][:, m, n * C:(n + 1) * C], wv[:, k, 4 * m + n],
                                                   xgT[:, e % 2, k], start=(k == 0), stop=(k == K - 1))
                    ins.then_inc(hid_ready, 1)

            def expert_out(e):
                if e >= 2:
                    pe.wait_ge(y_ready, e - 1)
                for n in range(NF):
                    if n % 4 == 0:
                        pe.wait_ge(gelu_ready, 2 * e + n // 4 + 1)
                    ins = nc.tensor.matmul(YB[e % 2][:, 0:D], hs[:, e % 2, n], w2_sb[:, e % NW, n],
                                           start=(n == 0), stop=(n == NF - 1))
                ins.then_inc(y_used, 1)

            slots_turn(0)
            slots_turn(1)
            hidden(0)
            for e in range(E):
                if e + 2 < E:
                    slots_turn(e + 2)
                if e + 1 < E:
                    hidden(e + 1)
                expert_out(e)


_INS = ['x', 'ctx_gu', 'ctx_d', 'g_xattn', 'g_ffn', 'w_gate', 'w1', 'w2']


def kernel(x, fside_BxS2xS2_0, ctx_1024, g_xattn, g_ffn, L0_ffn_w_gate, L0_ffn_w1, L0_ffn_w2):
    import numpy as _np
    import concourse.bacc as _bacc
    from concourse import mybir as _mybir
    from concourse.bass_utils import run_bass_kernel_spmd as _run

    nc = _bacc.Bacc("TRN2", target_bir_lowering=False, num_devices=1)
    given = [x, fside_BxS2xS2_0, ctx_1024, g_xattn, g_ffn, L0_ffn_w_gate, L0_ffn_w1, L0_ffn_w2]
    arrays, args = {}, []
    for name, a in zip(_INS, given):
        a = _np.ascontiguousarray(a)
        arrays[f"in_{name}"] = a
        args.append(nc.dram_tensor(f"in_{name}", a.shape, _mybir.dt.from_np(a.dtype), kind="ExternalInput").ap())
    tokens = x.shape[0] * x.shape[1]
    scratch = nc.dram_tensor("slot_rows", (tokens, x.shape[2] + 3 + L0_ffn_w_gate.shape[1]), _mybir.dt.float32,
                             kind="Internal").ap()
    out = nc.dram_tensor("out_0", tuple(x.shape), _mybir.dt.float32, kind="ExternalOutput").ap()
    gated_smoothquant_moe_kernel(nc, *args, scratch, out)
    r = _run(nc, [arrays], core_ids=[0])
    return r.results[0]["out_0"]
```

```python
import concourse.bass as bass
from concourse import mybir
from contextlib import ExitStack


def gated_smoothquant_moe_kernel(nc, x_in, ctx_in, down_in, g_xattn, g_ffn, w_gate, w1, w2, scratch, out):
    F32 = mybir.dt.float32
    BF16 = mybir.dt.bfloat16
    F32R = mybir.dt.float32r
    I32 = mybir.dt.int32
    ALU = mybir.AluOpType
    ACT = mybir.ActivationFunctionType
    AX = mybir.AxisListType.X

    P = 128
    B, T, D = x_in.shape
    I = down_in.shape[2]
    E, _, F = w1.shape
    J = T // P
    K = D // P
    C = B * T // E
    NF = F // P
    assert (T, D, I, C) == (256, 256, P, P) and ctx_in.shape[1] == 2 * I
    EPS, LN_EPS, QMAX = 1e-6, 1e-5, 127.0
    ROUND = 12582912.0
    DROPPED = 4096.0
    SHIFT, RSTD, TOKEN, LOGIT = D, D + 1, D + 2, D + 3
    ROW = LOGIT + E
    WARM = 28
    NW1, NW2 = 5, 5

    ctx = ExitStack()
    with ctx:
        def sb(name, shape, dt=F32):
            return ctx.enter_context(nc.sbuf_tensor(name, shape, dt))

        def ps(name, shape, dt=F32):
            return ctx.enter_context(nc.psum_tensor(name, shape, dt))

        def sem(name):
            return ctx.enter_context(nc.semaphore(name))

        x = sb("x", [P, B, J, D])
        cw = sb("cw", [P, B, J, D])
        dw = sb("dw", [P, B, K, I])
        wg = sb("wg", [P, K, E])
        ident = sb("ident", [P, P])
        identb = sb("identb", [P, P], BF16)
        upper = sb("upper", [P, P], BF16)
        upper_eq = sb("upper_eq", [P, P], BF16)
        ones = sb("ones", [P, P], BF16)
        rank = sb("rank", [P, J, E])
        powers = sb("powers", [P, 2, K])
        mhalf = sb("mhalf", [P, J])
        rbias = sb("rbias", [P, 1])
        unused = sb("unused", [P, 1])
        gates = sb("gates", [P, 2])
        tg = sb("tg", [P, 2])
        empty = sb("empty", [P, 1, ROW])
        wide_a = sb("wide_a", [P, B, 2 * K * T])
        wide_b = sb("wide_b", [P, B, 2 * K * T])
        rows_w = sb("rows_w", [P, B, J, D])
        ints = sb("ints", [P, B, 2 * J * D], BF16)
        intsT = sb("intsT", [P, B, 2 * K * T], BF16)
        scrow = sb("scrow", [P, B, T])
        xs1 = wide_a[:].rearrange("p b (c t) -> p b c t", c=2 * K)
        qf1 = wide_b[:].rearrange("p b (c d) -> p b c d", c=2 * J)
        xn = rows_w
        qb1 = ints[:].rearrange("p b (c d) -> p b c d", c=2 * J)
        qT1 = intsT[:].rearrange("p b (c t) -> p b c t", c=2 * K)
        xrow = scrow
        st1 = sb("st1", [P, B, J, 6])
        mv1 = sb("mv1", [P, B, J, 2])
        ve1 = sb("ve1", [P, B, J])
        rs1 = sb("rs1", [P, B, J])
        nm1 = sb("nm1", [P, B, J])
        sh1 = sb("sh1", [P, B, J])
        am1 = sb("am1", [P, B, 2 * K])
        rw1 = sb("rw1", [P, B, K])
        ra1 = sb("ra1", [P, B, K])
        sc1 = sb("sc1", [P, B, 2 * K])
        am2 = sb("am2", [P, B, 2 * J])
        q1s = sb("q1s", [P, B, 2 * J])
        q1r = sb("q1r", [P, B, 2 * J])
        g_sb = wide_a[:, :, 0:T]
        u_sb = wide_a[:, :, T:2 * T]
        sg = wide_a[:, :, 2 * T:3 * T]
        a_sb = wide_a[:, :, 3 * T:4 * T]
        aw = wide_b[:, :, 0:2 * T].rearrange("p b (c t) -> p b c t", c=2)
        qf2 = wide_b[:, :, 2 * T:4 * T].rearrange("p b (c i) -> p b c i", c=2 * J)
        qb2 = ints[:, :, 0:2 * J * I].rearrange("p b (c i) -> p b c i", c=2 * J)
        qT2 = intsT[:, :, 0:2 * T].rearrange("p b (c t) -> p b c t", c=2)
        drow = scrow
        y1 = rows_w
        amd = sb("amd", [P, B])
        rwd = sb("rwd", [P, B])
        ama = sb("ama", [P, B])
        ra2 = sb("ra2", [P, B])
        sc3 = sb("sc3", [P, B, 2])
        am4 = sb("am4", [P, B, 2 * J])
        q2s = sb("q2s", [P, B, 2 * J])
        q2r = sb("q2r", [P, B, 2 * J])
        q2g = sb("q2g", [P, B, J])
        row = sb("row", [P, B, J, ROW])
        st2 = sb("st2", [P, B, J, 6])
        mv2 = sb("mv2", [P, B, J, 2])
        ve2 = sb("ve2", [P, B, J])
        nm2 = sb("nm2", [P, B, J])
        xn2 = rows_w
        xn2T = wide_b[:, :, 0:K * T].rearrange("p b (k t) -> p b k t", k=K)
        lmax = sb("lmax", [P, B, J])
        prio = sb("prio", [P, B, J, E])
        pmax = sb("pmax", [P, B, J])
        base = sb("base", [P, B, J])
        onehot = sb("onehot", [P, B, J, E], BF16)
        locm = sb("locm", [P, B, J, E])
        loc = sb("loc", [P, B, J])
        over = sb("over", [P, B, J])
        slot = sb("slot", [P, B, J], I32)
        w1_sb = sb("w1_sb", [P, 3, K * F])
        w2_sb = sb("w2_sb", [P, 3, NF * D])
        gr = sb("gr", [P, E, ROW])
        gmax = sb("gmax", [P, E])
        lrel = sb("lrel", [P, E, E])
        ex = sb("ex", [P, E, E])
        zs = sb("zs", [P, E])
        zr = sb("zr", [P, E])
        gt = sb("gt", [P, E])
        w2p = sb("w2p", [P, 2, NF, 2, D], F32R)
        xg = rows_w[:, :, 0]
        xgT = rows_w[:, :, 1].rearrange("p x (k c) -> p x k c", k=K)
        hs = wide_a[:, 0:2].rearrange("p a (n c) -> p a n c", c=C)
        hh = sb("hh", [P, 2, NF, C], F32R)
        hl = sb("hl", [P, 2, NF, C], F32R)
        w1_place = [w1_sb[:, i] for i in range(3)] + [x[:].rearrange("p b j d -> p (b j d)"),
                                                      wide_a[:, 2:4].rearrange("p b c -> p (b c)")]
        w2_place = [w2_sb[:, i] for i in range(3)] + [cw[:].rearrange("p b j d -> p (b j d)"),
                                                      wide_b[:, 0:2].rearrange("p b c -> p (b c)")]
        assert len(w1_place) == NW1 and len(w2_place) == NW2
        yo = sb("yo", [P, 2, D])

        bk = [ps(f"bk{i}", [P, 2, 512]) for i in range(B)]
        HB = [bk[0], bk[1]]
        XT = [bk[2][:, 0, :], bk[2][:, 1, :]]
        YB = [bk[3][:, 0, :], bk[3][:, 1, :]]

        x_here = [sem(f"x_here{b}") for b in range(B)]
        cw_here = [sem(f"cw_here{b}") for b in range(B)]
        small_here = sem("small_here")
        wg_here = sem("wg_here")
        dw_here = sem("dw_here")
        scratch_clear = sem("scratch_clear")
        w1_here = [sem(f"w1_here{i}") for i in range(NW1)]
        w2_here = [sem(f"w2_here{i}") for i in range(NW2)]
        plain_out = sem("plain_out")
        w2high_ready, w2low_ready = sem("w2high_ready"), sem("w2low_ready")
        hhigh_ready, hlow_ready = sem("hhigh_ready"), sem("hlow_ready")
        rows_scattered = sem("rows_scattered")
        rows_here = sem("rows_here")
        rest_here = sem("rest_here")
        out_scattered = [sem("out_scattered0"), sem("out_scattered1")]
        consts = sem("consts")
        pool_c = sem("pool_c")
        dve_c = sem("dve_c")
        dve_consts = sem("dve_consts")
        tanh_ready = sem("tanh_ready")
        shift1_ready, shift2_ready = sem("shift1_ready"), sem("shift2_ready")
        var1_ready, rstd1_ready, xn_ready = sem("var1_ready"), sem("rstd1_ready"), sem("xn_ready")
        t1_ready, ratio1_ready = sem("t1_ready"), sem("ratio1_ready")
        scale1_ready = sem("scale1_ready")
        guard1_ready, guard2_ready = sem("guard1_ready"), sem("guard2_ready")
        scaled1, t2_ready = [sem("scaled1x"), sem("scaled1w")], [sem("t2x_ready"), sem("t2w_ready")]
        recip1_ready = sem("recip1_ready")
        quant1, rounded1 = [sem("quant1x"), sem("quant1w")], [sem("rounded1x"), sem("rounded1w")]
        t3_ready, moved1, row1_ready, row1_moved = sem("t3_ready"), sem("moved1"), sem("row1_ready"), sem("row1_moved")
        h_ready, gate_ready, up_ready = sem("h_ready"), sem("gate_ready"), sem("up_ready")
        silu_ready, act_ready = sem("silu_ready"), sem("act_ready")
        dT_ready, damax_ready = sem("dT_ready"), sem("damax_ready")
        ratio2_ready, scale2_ready = sem("ratio2_ready"), sem("scale2_ready")
        scaled2, t4_ready, recip2_ready = sem("scaled2"), sem("t4_ready"), sem("recip2_ready")
        quant2, rounded2, t5_ready, moved2 = sem("quant2"), sem("rounded2"), sem("t5_ready"), sem("moved2")
        row2_ready, row2_moved, o_ready, y1_ready = sem("row2_ready"), sem("row2_moved"), sem("o_ready"), sem("y1_ready")
        x1_ready, var2_ready, rstd2_ready, xn2_ready = sem("x1_ready"), sem("var2_ready"), sem("rstd2_ready"), sem("xn2_ready")
        t6_ready, moved3, logits_ready = sem("t6_ready"), sem("moved3"), sem("logits_ready")
        onehot_ready, loc_ready, slot_ready = sem("onehot_ready"), sem("loc_ready"), sem("slot_ready")
        exp_ready, lrel_ready = sem("exp_ready"), sem("lrel_ready")
        xg_ready, xT_ready, xgT_ready = sem("xg_ready"), sem("xT_ready"), sem("xgT_ready")
        hid_ready, gelu_ready, y_ready, y_used = sem("hid_ready"), sem("gelu_ready"), sem("y_ready"), sem("y_used")

        block = ctx.enter_context(nc.Block())

        @block.sync
        def _(sp):
            def load_x(b):
                sp.dma_start(x[:, b], x_in[b].rearrange("(p j) d -> p j d", j=J)).then_inc(x_here[b], 16)

            def load_cw(b):
                sp.dma_start(cw[:, b], ctx_in[b].rearrange("(j p) d -> p j d", p=P)).then_inc(cw_here[b], 16)

            load_x(0)
            load_x(1)
            load_cw(0)
            sp.dma_start(gates[:, 0:1], g_xattn.partition_broadcast(P)).then_inc(small_here, 16)
            sp.dma_start(gates[:, 1:2], g_ffn.partition_broadcast(P)).then_inc(small_here, 16)
            for b in range(1, B):
                if b + 1 < B:
                    load_x(b + 1)
                load_cw(b)
            sp.dma_start(dw[:], down_in.rearrange("b (k p) i -> p b k i", p=P)).then_inc(dw_here, 16)
            sp.dma_start(wg[:], w_gate.rearrange("(k p) e -> p k e", p=P)).then_inc(wg_here, 16)
            sp.wait_ge(consts, 2)
            sp.dma_start(scratch.rearrange("(e p) r -> p e r", p=P),
                         empty[:].to_broadcast([P, E, ROW])).then_inc(scratch_clear, 16)

            def load_w1(e):
                if e >= 1:
                    sp.wait_ge(w1_here[(e - 1) % NW1], 16 * ((e - 1) // NW1 + 1))
                if e >= NW1:
                    sp.wait_ge(hid_ready, 2 * (e - NW1 + 1))
                sp.dma_start(w1_place[e % NW1].rearrange("p (k f) -> p k f", k=K),
                             w1[e].rearrange("(p k) f -> p k f", k=K)).then_inc(w1_here[e % NW1], 16)

            def load_w2(e):
                if e >= 1:
                    sp.wait_ge(w2_here[(e - 1) % NW2], 16 * ((e - 1) // NW2 + 1))
                if e >= NW2:
                    sp.wait_ge(w2low_ready, e - NW2 + 1)
                sp.dma_start(w2_place[e % NW2].rearrange("p (n d) -> p n d", n=NF),
                             w2[e].rearrange("(p n) d -> p n d", n=NF)).then_inc(w2_here[e % NW2], 16)

            for e in range(3):
                load_w1(e)
                load_w2(e)
            sp.wait_ge(t1_ready, B)
            load_w2(3)
            for b in range(B):
                sp.wait_ge(x1_ready, b + 1)
                sp.dma_start(out[b].rearrange("(p j) d -> p j d", j=J), row[:, b, :, 0:D]).then_inc(plain_out, 16)
            load_w1(3)
            sp.wait_ge(rest_here, 16)
            for e in range(4, E):
                load_w1(e)
                load_w2(e)
            for n in range(2):
                sp.wait_ge(out_scattered[n], 16 * (E // 2))

        @block.gpsimd
        def _(pool):
            nc.gpsimd.memset(ident[:], 0.0).then_inc(pool_c, 1)
            nc.gpsimd.memset(upper[:], 1.0).then_inc(pool_c, 1)
            nc.gpsimd.memset(upper_eq[:], 1.0).then_inc(pool_c, 1)
            nc.gpsimd.memset(empty[:], 0.0).then_inc(pool_c, 1)
            nc.gpsimd.memset(identb[:], 0.0).then_inc(pool_c, 1)
            pool.wait_ge(pool_c, 5)
            nc.gpsimd.affine_select(out=ident[:], in_=ident[:], compare_op=ALU.not_equal, fill=1.0, base=0,
                                    pattern=[[-1, P]], channel_multiplier=1).then_inc(consts, 1)
            nc.gpsimd.iota(empty[:, :, TOKEN:TOKEN + 1].bitcast(I32), pattern=[[0, 1]], base=1 << 20,
                           channel_multiplier=0).then_inc(consts, 1)
            nc.gpsimd.affine_select(out=identb[:], in_=identb[:], compare_op=ALU.not_equal, fill=1.0, base=0,
                                    pattern=[[-1, P]], channel_multiplier=1).then_inc(consts, 1)
            nc.gpsimd.affine_select(out=upper[:], in_=upper[:], compare_op=ALU.is_gt, fill=0.0, base=0,
                                    pattern=[[1, P]], channel_multiplier=-1).then_inc(consts, 1)
            nc.gpsimd.affine_select(out=upper_eq[:], in_=upper_eq[:], compare_op=ALU.is_ge, fill=0.0, base=0,
                                    pattern=[[1, P]], channel_multiplier=-1).then_inc(consts, 1)
            nc.gpsimd.iota(rank[:], pattern=[[0, J], [-1, E]], base=E, channel_multiplier=0,
                           allow_small_or_imprecise_dtypes=True).then_inc(consts, 1)
            nc.gpsimd.iota(row[:, :, :, TOKEN:TOKEN + 1].bitcast(I32), pattern=[[T, B], [1, J]], base=0,
                           channel_multiplier=J).then_inc(consts, 1)

            def rstd1(b):
                pool.wait_ge(var1_ready, b + 1)
                nc.gpsimd.tensor_tensor(rs1[:, b], ve1[:, b], mhalf[:], ALU.pow).then_inc(rstd1_ready, 1)
                pool.wait_ge(rstd1_ready, b + 1)
                nc.gpsimd.tensor_tensor(sh1[:, b], nm1[:, b], rs1[:, b], ALU.mult).then_inc(shift1_ready, 1)

            def root_1(b):
                pool.wait_ge(ratio1_ready, b + 1)
                nc.gpsimd.tensor_scalar(ra1[:, b], ra1[:, b], EPS * EPS, None, ALU.max).then_inc(guard1_ready, 1)
                pool.wait_ge(guard1_ready, b + 1)
                nc.gpsimd.tensor_tensor(sc1[:, b].rearrange("p (a k) -> p a k", a=2),
                                        ra1[:, b].unsqueeze(1).to_broadcast([P, 2, K]), powers[:],
                                        ALU.pow).then_inc(scale1_ready, 1)

            def round1(b, a):
                pool.wait_ge(quant1[a], b + 1)
                nc.gpsimd.tensor_scalar(qb1[:, b, J * a:J * (a + 1)], qf1[:, b, J * a:J * (a + 1)], -ROUND, 1.0,
                                        ALU.add, ALU.mult).then_inc(rounded1[a], 1)

            def act_product(b):
                pool.wait_ge(silu_ready, b + 1)
                pool.wait_ge(up_ready, b + 1)
                nc.gpsimd.tensor_tensor(a_sb[:, b], sg[:, b], u_sb[:, b], ALU.mult).then_inc(act_ready, 1)

            def root_2(b):
                pool.wait_ge(ratio2_ready, b + 1)
                nc.gpsimd.tensor_scalar(ra2[:, b:b + 1], ra2[:, b:b + 1], EPS * EPS, None, ALU.max).then_inc(guard2_ready, 1)
                pool.wait_ge(guard2_ready, b + 1)
                nc.gpsimd.tensor_tensor(sc3[:, b], ra2[:, b:b + 1].to_broadcast([P, 2]), powers[:, :, 0],
                                        ALU.pow).then_inc(scale2_ready, 1)

            def round2(b):
                pool.wait_ge(quant2, b + 1)
                nc.gpsimd.tensor_scalar(qb2[:, b], qf2[:, b], -ROUND, 1.0, ALU.add, ALU.mult).then_inc(rounded2, 1)

            def residual(b):
                pool.wait_ge(y1_ready, b + 1)
                nc.gpsimd.tensor_tensor(row[:, b, :, 0:D], x[:, b], y1[:, b], ALU.add).then_inc(x1_ready, 1)

            def rstd2(b):
                pool.wait_ge(var2_ready, b + 1)
                nc.gpsimd.tensor_tensor(row[:, b, :, RSTD], ve2[:, b], mhalf[:], ALU.pow).then_inc(rstd2_ready, 1)
                pool.wait_ge(rstd2_ready, b + 1)
                nc.gpsimd.tensor_tensor(row[:, b, :, SHIFT], nm2[:, b], row[:, b, :, RSTD],
                                        ALU.mult).then_inc(shift2_ready, 1)

            def scatter(b):
                pool.wait_ge(slot_ready, b + 1)
                if b == 0:
                    pool.wait_ge(scratch_clear, 16)
                    pool.wait_ge(consts, 7)
                for j in range(J):
                    nc.gpsimd.indirect_dma_start(
                        scratch, bass.IndirectOffsetOnAxis(ap=slot[:, b, j:j + 1], axis=0), row[:, b, j, :], None,
                        bounds_check=E * C - 1, oob_is_err=False).then_inc(rows_scattered, 16)

            pool.wait_ge(dve_consts, 1)
            rstd1(0)
            rstd1(1)
            rstd1(2)
            rstd1(3)
            root_1(0)
            root_1(1)
            root_1(2)
            round1(0, 1)
            round1(0, 0)
            root_1(3)
            round1(1, 1)
            round1(1, 0)
            act_product(0)
            round1(2, 1)
            round1(2, 0)
            root_2(0)
            act_product(1)
            round1(3, 1)
            root_2(1)
            round1(3, 0)
            act_product(2)
            root_2(2)
            round2(0)
            act_product(3)
            root_2(3)
            residual(0)
            round2(1)
            round2(2)
            rstd2(0)
            residual(1)
            residual(2)
            round2(3)
            rstd2(1)
            rstd2(2)
            residual(3)
            rstd2(3)
            scatter(0)
            scatter(1)
            scatter(2)
            scatter(3)

            out_rows = out.rearrange("b t d -> (b t) d")
            for e in range(E):
                pool.wait_ge(y_ready, e + 1)
                if e == 0:
                    pool.wait_ge(plain_out, 16 * B)
                nc.gpsimd.indirect_dma_start(
                    out_rows, bass.IndirectOffsetOnAxis(ap=gr[:, e, TOKEN:TOKEN + 1].bitcast(I32), axis=0),
                    yo[:, e % 2, :], None, bounds_check=B * T - 1, oob_is_err=False).then_inc(out_scattered[e % 2], 16)

        @block.scalar
        def _(act):
            act.wait_ge(dve_consts, 1)
            nc.scalar.activation(unused[:], rbias[:], ACT.Silu)
            act.wait_ge(small_here, 32)
            nc.scalar.activation(tg[:], gates[:], ACT.Tanh).then_inc(tanh_ready, 1)

            def norm1(b):
                act.wait_ge(shift1_ready, b + 1)
                for j in range(J):
                    last = nc.scalar.activation(xn[:, b, j], x[:, b, j], ACT.Identity, scale=rs1[:, b, j:j + 1],
                                                bias=sh1[:, b, j:j + 1])
                last.then_inc(xn_ready, 1)

            def norm2(b):
                act.wait_ge(shift2_ready, b + 1)
                for j in range(J):
                    last = nc.scalar.activation(xn2[:, b, j], row[:, b, j, 0:D], ACT.Identity,
                                                scale=row[:, b, j, RSTD:RSTD + 1],
                                                bias=row[:, b, j, SHIFT:SHIFT + 1])
                last.then_inc(xn2_ready, 1)

            def scale1(b, a):
                act.wait_ge(scale1_ready, b + 1)
                for k in range(K):
                    c = a * K + k
                    last = nc.scalar.activation(xs1[:, b, c], bk[b][:, a, k * T:(k + 1) * T],
                                                ACT.Identity, scale=sc1[:, b, c:c + 1])
                last.then_inc(scaled1[a], 1)

            def quantise1(b, a):
                act.wait_ge(recip1_ready, b + 1)
                for j in range(J):
                    c = a * J + j
                    last = nc.scalar.activation(qf1[:, b, c], bk[b][:, a, j * D:(j + 1) * D],
                                                ACT.Identity, scale=q1r[:, b, c:c + 1], bias=rbias[:, 0:1])
                last.then_inc(quant1[a], 1)

            def move_row1(b):
                act.wait_ge(row1_ready, b + 1)
                nc.scalar.activation(xrow[:, b], bk[b][:, 1, 0:T], ACT.Copy).then_inc(row1_moved, 1)

            def move1(b):
                act.wait_ge(t3_ready, b + 1)
                nc.scalar.activation(intsT[:, b].bitcast(F32), bk[b][:, 0, :], ACT.Copy).then_inc(moved1, 1)

            def silu(b):
                act.wait_ge(gate_ready, b + 1)
                nc.scalar.activation(sg[:, b], g_sb[:, b], ACT.Silu).then_inc(silu_ready, 1)

            def scale2(b):
                act.wait_ge(scale2_ready, b + 1)
                nc.scalar.activation(aw[:, b, 0], a_sb[:, b], ACT.Identity, scale=sc3[:, b, 0:1])
                nc.scalar.activation(aw[:, b, 1], bk[b][:, 1, 0:D], ACT.Identity,
                                     scale=sc3[:, b, 1:2]).then_inc(scaled2, 1)

            def quantise2(b):
                act.wait_ge(recip2_ready, b + 1)
                for c in range(2 * J):
                    last = nc.scalar.activation(qf2[:, b, c], bk[b][:, 0, c * I:(c + 1) * I], ACT.Identity,
                                                scale=q2r[:, b, c:c + 1], bias=rbias[:, 0:1])
                last.then_inc(quant2, 1)

            def move_row2(b):
                act.wait_ge(row2_ready, b + 1)
                nc.scalar.activation(drow[:, b], bk[b][:, 1, 0:D], ACT.Copy).then_inc(row2_moved, 1)

            def move2(b):
                act.wait_ge(t5_ready, b + 1)
                nc.scalar.activation(intsT[:, b, 0:2 * T].bitcast(F32), bk[b][:, 0, 0:T],
                                     ACT.Copy).then_inc(moved2, 1)

            def move3(b):
                act.wait_ge(t6_ready, b + 1)
                nc.scalar.activation(wide_b[:, b, 0:K * T], bk[b][:, 0, :], ACT.Copy).then_inc(moved3, 1)

            def split_high(e):
                act.wait_ge(w2_here[e % NW2], 16 * (e // NW2 + 1))
                if e >= 2:
                    act.wait_ge(y_used, e - 1)
                w2v = w2_place[e % NW2].rearrange("p (n d) -> p n d", n=NF)
                for n in (0, NF // 2):
                    last = nc.scalar.activation(w2p[:, e % 2, n:n + NF // 2, 0], w2v[:, n:n + NF // 2], ACT.Copy)
                last.then_inc(w2high_ready, 1)

            norm1(0)
            norm1(1)
            norm1(2)
            norm1(3)
            scale1(0, 1)
            scale1(0, 0)
            scale1(1, 1)
            scale1(1, 0)
            scale1(2, 1)
            scale1(2, 0)
            quantise1(0, 1)
            quantise1(0, 0)
            move_row1(0)
            quantise1(1, 0)
            quantise1(1, 1)
            move1(0)
            scale1(3, 1)
            scale1(3, 0)
            silu(0)
            quantise1(2, 1)
            move1(1)
            quantise1(2, 0)
            move_row1(1)
            quantise1(3, 1)
            silu(1)
            move_row1(2)
            move1(2)
            scale2(0)
            quantise1(3, 0)
            move_row1(3)
            silu(2)
            scale2(1)
            move1(3)
            quantise2(0)
            silu(3)
            scale2(2)
            move_row2(0)
            move2(0)
            quantise2(1)
            move_row2(1)
            scale2(3)
            quantise2(2)
            move2(1)
            move_row2(2)
            move2(2)
            norm2(0)
            quantise2(3)
            move3(0)
            move_row2(3)
            move2(3)
            norm2(1)
            norm2(2)
            move3(1)
            move3(2)
            norm2(3)
            move3(3)
            split_high(0)
            split_high(1)

            sc_rows = scratch.rearrange("(e p) r -> p e r", p=P)
            act.wait_ge(rows_scattered, 16 * B * J)
            act.dma_start(gr[:, 0:1], sc_rows[:, 0:1]).then_inc(rows_here, 16)
            act.dma_start(gr[:, 1:E], sc_rows[:, 1:E]).then_inc(rest_here, 16)
            act.wait_ge(lrel_ready, 1)
            nc.scalar.activation(ex[:], lrel[:], ACT.Exp).then_inc(exp_ready, 1)
            for e in range(E):
                for m in range(2):
                    act.wait_ge(hid_ready, 2 * e + m + 1)
                    if e >= 2:
                        act.wait_ge(y_used, e - 1)
                    part = slice(4 * m, 4 * m + 4)
                    nc.scalar.activation(hs[:, e % 2, part].rearrange("p n c -> p (n c)"),
                                         HB[e % 2][:, m, :], ACT.Gelu_apprx_tanh).then_inc(gelu_ready, 1)
                    act.wait_ge(gelu_ready, 2 * e + m + 1)
                    nc.scalar.activation(hh[:, e % 2, part], hs[:, e % 2, part], ACT.Copy).then_inc(hhigh_ready, 1)
                if e >= 1 and e + 1 < E:
                    split_high(e + 1)

        @block.vector
        def _(dve):
            chain = [0]

            def mark(ins):
                chain[0] += 1
                ins.then_inc(dve_c, 1)
                return chain[0]

            def link(ins):
                dve.wait_ge(dve_c, mark(ins))

            nc.vector.memset(powers[:, 0], -0.5)
            nc.vector.memset(powers[:, 1], 0.5)
            nc.vector.memset(mhalf[:], -0.5)
            nc.vector.memset(ones[:], 1.0)
            nc.vector.memset(rbias[:], ROUND).then_inc(dve_consts, 1)

            def stats1(b):
                dve.wait_ge(x_here[b], 16)
                done = [mark(nc.vector.bn_stats(st1[:, b, j], x[:, b, j])) for j in range(J)]
                for j in range(J):
                    dve.wait_ge(dve_c, done[j])
                    ins = nc.vector.bn_aggr(mv1[:, b, j], st1[:, b, j])
                link(ins)
                nc.vector.tensor_scalar(nm1[:, b], mv1[:, b, :, 0], -1.0, None, ALU.mult)
                nc.vector.tensor_scalar(ve1[:, b], mv1[:, b, :, 1], LN_EPS, None, ALU.add).then_inc(var1_ready, 1)

            def amax1(b):
                dve.wait_ge(t1_ready, b + 1)
                link(nc.vector.tensor_reduce(am1[:, b], bk[b][:].rearrange("p a (k t) -> p (a k) t", k=K), AX, ALU.max,
                                             apply_absolute_value=True))
                link(nc.vector.tensor_scalar(am1[:, b], am1[:, b], EPS, None, ALU.max))
                link(nc.vector.reciprocal(rw1[:, b], am1[:, b, K:2 * K]))
                nc.vector.tensor_tensor(ra1[:, b], am1[:, b, 0:K], rw1[:, b], ALU.mult).then_inc(ratio1_ready, 1)

            def scales1(b):
                for a in range(2):
                    dve.wait_ge(t2_ready[a], b + 1)
                    ins = nc.vector.tensor_reduce(am2[:, b, a * J:(a + 1) * J],
                                                  bk[b][:, a, :].rearrange("p (j d) -> p j d", j=J),
                                                  AX, ALU.max, apply_absolute_value=True)
                link(ins)
                link(nc.vector.tensor_scalar(q1s[:, b], am2[:, b], EPS, 1.0 / QMAX, ALU.max, ALU.mult))
                nc.vector.reciprocal(q1r[:, b], q1s[:, b]).then_inc(recip1_ready, 1)

            def gate_up(b):
                dve.wait_ge(h_ready, b + 1)
                dve.wait_ge(row1_moved, b + 1)
                for h, (dst, done) in enumerate(((g_sb, gate_ready), (u_sb, up_ready))):
                    nc.vector.scalar_tensor_tensor(out=dst[:, b], in0=bk[b][:, 0, h * T:(h + 1) * T],
                                                   scalar=q1s[:, b, J + h:J + h + 1], in1=xrow[:, b],
                                                   op0=ALU.mult, op1=ALU.mult).then_inc(done, 1)

            def down_amax(b):
                dve.wait_ge(dT_ready, b + 1)
                link(nc.vector.tensor_reduce(amd[:, b:b + 1], bk[b][:, 1, 0:D], AX, ALU.max, apply_absolute_value=True))
                link(nc.vector.tensor_scalar(amd[:, b:b + 1], amd[:, b:b + 1], EPS, None, ALU.max))
                mark(nc.vector.reciprocal(rwd[:, b:b + 1], amd[:, b:b + 1]))

            def amax2(b):
                dve.wait_ge(act_ready, b + 1)
                link(nc.vector.tensor_reduce(ama[:, b:b + 1], a_sb[:, b], AX, ALU.max, apply_absolute_value=True))
                nc.vector.tensor_scalar(ra2[:, b:b + 1], ama[:, b:b + 1], EPS, rwd[:, b:b + 1], ALU.max,
                                        ALU.mult).then_inc(ratio2_ready, 1)

            q2g_written = {}

            def scales2(b):
                dve.wait_ge(t4_ready, b + 1)
                link(nc.vector.tensor_reduce(am4[:, b], bk[b][:, 0, :].rearrange("p (c i) -> p c i", i=I), AX, ALU.max,
                                             apply_absolute_value=True))
                link(nc.vector.tensor_scalar(q2s[:, b], am4[:, b], EPS, 1.0 / QMAX, ALU.max, ALU.mult))
                nc.vector.reciprocal(q2r[:, b], q2s[:, b]).then_inc(recip2_ready, 1)
                if b == 0:
                    dve.wait_ge(tanh_ready, 1)
                q2g_written[b] = mark(nc.vector.tensor_scalar(q2g[:, b], q2s[:, b, 0:J], tg[:, 0:1], None, ALU.mult))

            def expert_out(b):
                dve.wait_ge(o_ready, b + 1)
                dve.wait_ge(row2_moved, b + 1)
                dve.wait_ge(dve_c, q2g_written[b])
                for j in range(J):
                    ins = nc.vector.scalar_tensor_tensor(out=y1[:, b, j], in0=bk[b][:, 0, j * D:(j + 1) * D],
                                                         scalar=q2g[:, b, j:j + 1], in1=drow[:, b],
                                                         op0=ALU.mult, op1=ALU.mult)
                ins.then_inc(y1_ready, 1)

            def stats2(b):
                dve.wait_ge(x1_ready, b + 1)
                done = [mark(nc.vector.bn_stats(st2[:, b, j], row[:, b, j, 0:D])) for j in range(J)]
                for j in range(J):
                    dve.wait_ge(dve_c, done[j])
                    ins = nc.vector.bn_aggr(mv2[:, b, j], st2[:, b, j])
                link(ins)
                nc.vector.tensor_scalar(nm2[:, b], mv2[:, b, :, 0], -1.0, None, ALU.mult)
                nc.vector.tensor_scalar(ve2[:, b], mv2[:, b, :, 1], LN_EPS, None, ALU.add).then_inc(var2_ready, 1)

            def choose(b):
                dve.wait_ge(logits_ready, b + 1)
                if b == 0:
                    dve.wait_ge(consts, 7)
                lg = bk[b][:, 1, 0:J * E].rearrange("p (j e) -> p j e", e=E)
                top = mark(nc.vector.tensor_reduce(lmax[:, b], lg, AX, ALU.max))
                nc.vector.tensor_copy(row[:, b, :, LOGIT:ROW], lg)
                dve.wait_ge(dve_c, top)
                for j in range(J):
                    ins = nc.vector.scalar_tensor_tensor(out=prio[:, b, j], in0=lg[:, j], scalar=lmax[:, b, j:j + 1],
                                                         in1=rank[:, j], op0=ALU.is_ge, op1=ALU.mult)
                link(ins)
                link(nc.vector.tensor_reduce(pmax[:, b], prio[:, b], AX, ALU.max))
                nc.vector.tensor_tensor(onehot[:, b], prio[:, b], pmax[:, b].unsqueeze(2).to_broadcast([P, J, E]),
                                        ALU.is_equal).then_inc(onehot_ready, 1)
                nc.vector.tensor_scalar(base[:, b], pmax[:, b], -float(C), float(C * E), ALU.mult, ALU.add)

            def place(b):
                dve.wait_ge(loc_ready, b + 1)
                dve.wait_ge(onehot_ready, b + 1)
                link(nc.vector.tensor_tensor(locm[:, b], bk[b][:, 1, J * E:2 * J * E].rearrange("p (j e) -> p j e", e=E),
                                             onehot[:, b], ALU.mult))
                link(nc.vector.tensor_reduce(loc[:, b], locm[:, b], AX, ALU.add))
                link(nc.vector.tensor_scalar(over[:, b], loc[:, b], float(C), DROPPED, ALU.is_ge, ALU.mult))
                for j in range(J):
                    ins = nc.vector.scalar_tensor_tensor(out=slot[:, b, j:j + 1], in0=loc[:, b, j:j + 1],
                                                         scalar=base[:, b, j:j + 1], in1=over[:, b, j:j + 1],
                                                         op0=ALU.add, op1=ALU.add)
                ins.then_inc(slot_ready, 1)

            def split_low(e):
                dve.wait_ge(w2high_ready, e + 1)
                w2v = w2_place[e % NW2].rearrange("p (n d) -> p n d", n=NF)
                for n in (0, NF // 2):
                    part = slice(n, n + NF // 2)
                    last = nc.vector.tensor_tensor(w2p[:, e % 2, part, 1], w2v[:, part],
                                                   w2p[:, e % 2, part, 0].bitcast(F32), ALU.subtract)
                last.then_inc(w2low_ready, 1)

            def hidden_low(e):
                for m in range(2):
                    dve.wait_ge(hhigh_ready, 2 * e + m + 1)
                    part = slice(4 * m, 4 * m + 4)
                    nc.vector.tensor_tensor(hl[:, e % 2, part], hs[:, e % 2, part],
                                            hh[:, e % 2, part].bitcast(F32), ALU.subtract).then_inc(hlow_ready, 1)

            stats1(0)
            stats1(1)
            stats1(2)
            stats1(3)
            amax1(0)
            amax1(1)
            amax1(2)
            scales1(0)
            scales1(1)
            amax1(3)
            scales1(2)
            gate_up(0)
            down_amax(0)
            scales1(3)
            amax2(0)
            gate_up(1)
            down_amax(1)
            amax2(1)
            down_amax(2)
            gate_up(2)
            scales2(0)
            amax2(2)
            down_amax(3)
            gate_up(3)
            scales2(1)
            amax2(3)
            expert_out(0)
            scales2(2)
            stats2(0)
            scales2(3)
            expert_out(1)
            expert_out(2)
            stats2(1)
            stats2(2)
            expert_out(3)
            choose(0)
            stats2(3)
            choose(1)
            place(0)
            choose(2)
            place(1)
            place(2)
            choose(3)
            place(3)
            split_low(0)
            split_low(1)

            def expert_in(e):
                dve.wait_ge(rows_here if e == 0 else rest_here, 16)
                if e >= B:
                    dve.wait_ge(xT_ready, e - B + 1)
                nc.vector.tensor_scalar(xg[:, e % B], gr[:, e, 0:D], gr[:, e, RSTD:RSTD + 1],
                                        gr[:, e, SHIFT:SHIFT + 1], ALU.mult, ALU.add).then_inc(xg_ready, 1)

            def expert_turned(e):
                dve.wait_ge(xT_ready, e + 1)
                if e >= B:
                    dve.wait_ge(hid_ready, 2 * (e - B + 1))
                nc.vector.tensor_copy(xgT[:, e % B].rearrange("p k c -> p (k c)"),
                                      XT[e % 2][:, 0:K * C]).then_inc(xgT_ready, 1)

            def expert_add(e):
                dve.wait_ge(y_used, e + 1)
                if e >= 2:
                    dve.wait_ge(out_scattered[e % 2], 16 * (e // 2))
                link(nc.vector.scalar_tensor_tensor(out=yo[:, e % 2], in0=YB[e % 2][:, 0:D], scalar=gt[:, e:e + 1],
                                                    in1=gr[:, e, 0:D], op0=ALU.mult, op1=ALU.add))
                nc.vector.scalar_tensor_tensor(out=yo[:, e % 2], in0=YB[e % 2][:, D:2 * D], scalar=gt[:, e:e + 1],
                                               in1=yo[:, e % 2], op0=ALU.mult, op1=ALU.add).then_inc(y_ready, 1)

            expert_in(0)
            expert_turned(0)
            expert_in(1)
            link(nc.vector.tensor_reduce(gmax[:], gr[:, :, LOGIT:ROW], AX, ALU.max))
            nc.vector.tensor_tensor(lrel[:], gr[:, :, LOGIT:ROW], gmax[:].unsqueeze(2).to_broadcast([P, E, E]),
                                    ALU.subtract).then_inc(lrel_ready, 1)
            expert_turned(1)
            expert_in(2)
            expert_turned(2)
            dve.wait_ge(exp_ready, 1)
            link(nc.vector.tensor_reduce(zs[:], ex[:], AX, ALU.add))
            link(nc.vector.reciprocal(zr[:], zs[:]))
            link(nc.vector.tensor_scalar(gt[:], zr[:], tg[:, 1:2], None, ALU.mult))
            expert_in(3)
            hidden_low(0)
            for e in range(E):
                if e + 3 < E:
                    expert_turned(e + 3)
                if e + 1 < E:
                    hidden_low(e + 1)
                expert_add(e)
                if e + 4 < E:
                    expert_in(e + 4)
                if e + 2 < E:
                    split_low(e + 2)

        @block.tensor
        def _(pe):
            pe.wait_ge(consts, 1)

            def keep_warm(n):
                for _ in range(n):
                    nc.tensor.matmul(HB[0][:, 0, :], upper[:], intsT[:, 0, 0:512], start=True, stop=True)

            def turn1(b):
                pe.wait_ge(cw_here[b], 16)
                for a, src in ((1, cw), (0, xn)):
                    if a == 0:
                        pe.wait_ge(xn_ready, b + 1)
                    for k in range(K):
                        for j in range(J):
                            ins = nc.tensor.transpose(bk[b][:, a, k * T + j * P:k * T + (j + 1) * P],
                                                      src[:, b, j, k * P:(k + 1) * P], ident[:])
                ins.then_inc(t1_ready, 1)

            def turn2(b, a):
                pe.wait_ge(scaled1[a], b + 1)
                for j in range(J):
                    for k in range(K):
                        ins = nc.tensor.transpose(bk[b][:, a, j * D + k * P:j * D + (k + 1) * P],
                                                  xs1[:, b, a * K + k, j * P:(j + 1) * P], ident[:])
                ins.then_inc(t2_ready[a], 1)

            def rows1(b):
                pe.wait_ge(quant1[1], b + 1)
                for j in range(J):
                    ins = nc.tensor.matmul(bk[b][:, 1, j * P:(j + 1) * P], q1s[:, b, j:j + 1].to_broadcast([P, P]),
                                           ident[:], start=True, stop=True)
                ins.then_inc(row1_ready, 1)

            def turn3(b):
                pe.wait_ge(rounded1[0], b + 1)
                pe.wait_ge(rounded1[1], b + 1)
                if b == 0:
                    pe.wait_ge(consts, 3)
                t3 = bk[b][:, 0, :].bitcast(BF16)
                for a in range(2):
                    for k in range(K):
                        for j in range(J):
                            o = (a * K + k) * T + j * P
                            ins = nc.tensor.transpose(t3[:, o:o + P], qb1[:, b, a * J + j, k * P:(k + 1) * P],
                                                      identb[:])
                ins.then_inc(t3_ready, 1)

            def product1(b):
                pe.wait_ge(moved1, b + 1)
                for h in range(2):
                    for k in range(K):
                        ins = nc.tensor.matmul(bk[b][:, 0, h * T:(h + 1) * T], qT1[:, b, K + k, h * P:(h + 1) * P],
                                               qT1[:, b, k, :], start=(k == 0), stop=(k == K - 1))
                ins.then_inc(h_ready, 1)

            def down_turn(b):
                pe.wait_ge(dw_here, 16)
                pe.wait_ge(row1_moved, b + 1)
                for k in range(K):
                    ins = nc.tensor.transpose(bk[b][:, 1, k * P:(k + 1) * P], dw[:, b, k], ident[:])
                ins.then_inc(dT_ready, 1)

            def turn4(b):
                pe.wait_ge(scaled2, b + 1)
                for a in range(2):
                    for j in range(J):
                        c = a * J + j
                        ins = nc.tensor.transpose(bk[b][:, 0, c * I:(c + 1) * I], aw[:, b, a, j * P:(j + 1) * P],
                                                  ident[:])
                ins.then_inc(t4_ready, 1)

            def rows2(b):
                pe.wait_ge(recip2_ready, b + 1)
                for k in range(K):
                    ins = nc.tensor.matmul(bk[b][:, 1, k * P:(k + 1) * P],
                                           q2s[:, b, J + k:J + k + 1].to_broadcast([P, P]),
                                           ident[:], start=True, stop=True)
                ins.then_inc(row2_ready, 1)

            def turn5(b):
                pe.wait_ge(rounded2, b + 1)
                t5 = bk[b][:, 0, :].bitcast(BF16)
                for c in range(2 * J):
                    ins = nc.tensor.transpose(t5[:, c * P:(c + 1) * P], qb2[:, b, c], identb[:])
                ins.then_inc(t5_ready, 1)

            def product2(b):
                pe.wait_ge(moved2, b + 1)
                for j in range(J):
                    ins = nc.tensor.matmul(bk[b][:, 0, j * D:(j + 1) * D], qT2[:, b, 0, j * P:(j + 1) * P],
                                           qT2[:, b, 1, :], start=True, stop=True)
                ins.then_inc(o_ready, 1)

            def turn6(b):
                pe.wait_ge(xn2_ready, b + 1)
                for k in range(K):
                    for j in range(J):
                        ins = nc.tensor.transpose(bk[b][:, 0, k * T + j * P:k * T + (j + 1) * P],
                                                  xn2[:, b, j, k * P:(k + 1) * P], ident[:])
                ins.then_inc(t6_ready, 1)

            def logits(b):
                pe.wait_ge(moved3, b + 1)
                if b == 0:
                    pe.wait_ge(wg_here, 16)
                for j in range(J):
                    for k in range(K):
                        ins = nc.tensor.matmul(bk[b][:, 1, j * E:(j + 1) * E], xn2T[:, b, k, j * P:(j + 1) * P],
                                               wg[:, k], start=(k == 0), stop=(k == K - 1))
                ins.then_inc(logits_ready, 1)

            def positions(b):
                pe.wait_ge(onehot_ready, b + 1)
                if b == 0:
                    pe.wait_ge(consts, 7)
                for j in range(J):
                    dst = bk[b][:, 1, (J + j) * E:(J + j + 1) * E]
                    terms = [(ones, onehot[:, bb, jj]) for bb in range(b) for jj in range(J)]
                    terms += [(upper_eq if jj < j else upper, onehot[:, b, jj]) for jj in range(J)]
                    for n, (tri, hot) in enumerate(terms):
                        ins = nc.tensor.matmul(dst, tri[:], hot, start=(n == 0), stop=(n == len(terms) - 1))
                ins.then_inc(loc_ready, 1)

            turn1(0)
            turn1(1)
            turn1(2)
            turn2(0, 1)
            turn1(3)
            turn2(0, 0)
            turn2(1, 1)
            turn2(1, 0)
            rows1(0)
            turn2(2, 0)
            turn3(0)
            turn2(2, 1)
            down_turn(0)
            rows1(1)
            product1(0)
            turn3(1)
            turn2(3, 0)
            turn2(3, 1)
            rows1(2)
            product1(1)
            down_turn(1)
            turn3(2)
            rows1(3)
            down_turn(2)
            product1(2)
            turn4(0)
            down_turn(3)
            turn3(3)
            turn4(1)
            product1(3)
            rows2(0)
            turn5(0)
            product2(0)
            turn4(2)
            rows2(1)
            turn4(3)
            turn5(1)
            product2(1)
            rows2(2)
            turn5(2)
            product2(2)
            rows2(3)
            turn6(0)
            turn5(3)
            logits(0)
            product2(3)
            turn6(1)
            turn6(2)
            positions(0)
            logits(1)
            logits(2)
            turn6(3)
            positions(1)
            positions(2)
            logits(3)
            positions(3)

            def slots_turn(e):
                pe.wait_ge(xg_ready, e + 1)
                if e == 0:
                    pe.wait_ge(slot_ready, B)
                if e >= 2:
                    pe.wait_ge(xgT_ready, e - 1)
                xv = xg[:, e % B].rearrange("p (f k) -> p k f", k=K)
                for k in range(K):
                    ins = nc.tensor.transpose(XT[e % 2][:, k * C:(k + 1) * C], xv[:, k], ident[:])
                ins.then_inc(xT_ready, 1)

            def hidden(e, m):
                if m == 0:
                    pe.wait_ge(xgT_ready, e + 1)
                    pe.wait_ge(w1_here[e % NW1], 16 * (e // NW1 + 1))
                wv = w1_place[e % NW1].rearrange("p (k f n) -> p k n f", k=K, n=NF)
                if e >= 2:
                    pe.wait_ge(gelu_ready, 2 * (e - 2) + m + 1)
                for n in range(4):
                    for k in range(K):
                        ins = nc.tensor.matmul(HB[e % 2][:, m, n * C:(n + 1) * C], wv[:, k, 4 * m + n],
                                               xgT[:, e % B, k], start=(k == 0), stop=(k == K - 1))
                ins.then_inc(hid_ready, 1)

            def expert_out(e):
                if e >= 2:
                    pe.wait_ge(y_ready, e - 1)
                pe.wait_ge(w2low_ready, e + 1)
                for n in range(NF):
                    if n % 4 == 0:
                        pe.wait_ge(hlow_ready, 2 * e + n // 4 + 1)
                    nc.tensor.matmul(YB[e % 2], hh[:, e % 2, n], w2p[:, e % 2, n].rearrange("p a d -> p (a d)"),
                                     start=(n == 0), stop=False)
                    ins = nc.tensor.matmul(YB[e % 2][:, 0:D], hl[:, e % 2, n], w2p[:, e % 2, n, 0],
                                           start=False, stop=(n == NF - 1))
                ins.then_inc(y_used, 1)

            keep_warm(WARM)
            slots_turn(0)
            hidden(0, 0)
            slots_turn(1)
            hidden(0, 1)
            slots_turn(2)
            for e in range(E):
                if e + 1 < E:
                    hidden(e + 1, 0)
                if e + 3 < E:
                    slots_turn(e + 3)
                if e + 1 < E:
                    hidden(e + 1, 1)
                expert_out(e)


_INS = ['x', 'ctx_gu', 'ctx_d', 'g_xattn', 'g_ffn', 'w_gate', 'w1', 'w2']


def kernel(x, fside_BxS2xS2_0, ctx_1024, g_xattn, g_ffn, L0_ffn_w_gate, L0_ffn_w1, L0_ffn_w2):
    import numpy as _np
    import concourse.bacc as _bacc
    from concourse import mybir as _mybir
    from concourse.bass_utils import run_bass_kernel_spmd as _run

    nc = _bacc.Bacc("TRN2", target_bir_lowering=False, num_devices=1)
    given = [x, fside_BxS2xS2_0, ctx_1024, g_xattn, g_ffn, L0_ffn_w_gate, L0_ffn_w1, L0_ffn_w2]
    arrays, args = {}, []
    for name, a in zip(_INS, given):
        a = _np.ascontiguousarray(a)
        arrays[f"in_{name}"] = a
        args.append(nc.dram_tensor(f"in_{name}", a.shape, _mybir.dt.from_np(a.dtype), kind="ExternalInput").ap())
    tokens = x.shape[0] * x.shape[1]
    scratch = nc.dram_tensor("slot_rows", (tokens, x.shape[2] + 3 + L0_ffn_w_gate.shape[1]), _mybir.dt.float32,
                             kind="Internal").ap()
    out = nc.dram_tensor("out_0", tuple(x.shape), _mybir.dt.float32, kind="ExternalOutput").ap()
    gated_smoothquant_moe_kernel(nc, *args, scratch, out)
    r = _run(nc, [arrays], core_ids=[0])
    return r.results[0]["out_0"]
```
